# Optimizing a Trainium2 kernel written in Bass

```python
import numpy as np
import jax
import jax.numpy as jnp

def _softmax(x, axis=-1):
    return jax.nn.softmax(x, axis=axis)

def _gelu(x):
    return jax.nn.gelu(x, approximate=True)

def _silu(x):
    return jax.nn.silu(x)

def _sigmoid(x):
    return jax.nn.sigmoid(x)

def _layernorm(x, axis=-1, eps=1e-05):
    m = jnp.mean(x, axis=axis, keepdims=True)
    v = jnp.var(x, axis=axis, keepdims=True)
    return (x - m) / jnp.sqrt(v + eps)

def _scatter_add(tgt, idx, src, axis=0):
    return tgt.at[idx].add(src)

def _segment_sum(src, seg, n):
    return jax.ops.segment_sum(src, seg, n)
kernel_name = 'mk_xattn_ffn_d1_seqx_r8_6ff82c'

def setup_inputs(seed: int=0):
    np.random.seed(seed)
    _w = jnp.asarray

    def _rec_inputs():
        import jax
        import jax.numpy as jnp
        _rk = jax.random.key(seed)
        x = -0.0002928 + 1 * jax.random.normal(jax.random.fold_in(_rk, 1), (16, 256, 128), jnp.float32)
        _lenS = 256 - jax.random.randint(jax.random.fold_in(_rk, 7), (16,), 0, max(1, 256 // 4) + 1, jnp.int32)
        _lenS2 = 1601 - jax.random.randint(jax.random.fold_in(_rk, 8), (16,), 0, max(1, 1601 // 4) + 1, jnp.int32)
        _ctx_1024P = jax.random.normal(jax.random.fold_in(_rk, 11), (16, 16, 128), jnp.float32)
        _ctx_1024c = jax.random.dirichlet(jax.random.fold_in(_rk, 511), 0.3 * jnp.ones((16,), jnp.float32), (16, 1601))
        _ctx_1024t = jnp.einsum('bsk,bkd->bsd', _ctx_1024c, _ctx_1024P)
        _ctx_1024t = _ctx_1024t * jax.lax.rsqrt(jnp.mean(jnp.square(_ctx_1024t)) + 1e-12) * 0.953939
        ctx_1024 = -1.39393e-06 + 0.999914 * (_ctx_1024t + 0.3 * jax.random.normal(jax.random.fold_in(_rk, 611), (16, 1601, 128), jnp.float32))
        return (x, ctx_1024)
    x, ctx_1024 = _rec_inputs()

    def _L0_xattn_setup():
        import jax, jax.numpy as jnp
        import numpy as np
        DIM = 128
        NUM_HEAD = 16
        DIM_HEAD = DIM // NUM_HEAD
        key = jax.random.key(seed)
        ks = jax.random.split(key, 11)
        B, S = (2, 256)
        s = 1.0 / np.sqrt(DIM)
        return {'query': jax.random.normal(ks[0], (B, S, DIM), jnp.float32), 'key': jax.random.normal(ks[1], (B, S, DIM), jnp.float32), 'value': jax.random.normal(ks[2], (B, S, DIM), jnp.float32), 'wq': jax.random.normal(ks[3], (DIM, DIM), jnp.float32) * s, 'bq': jax.random.normal(ks[4], (DIM,), jnp.float32) * s, 'wk': jax.random.normal(ks[5], (DIM, DIM), jnp.float32) * s, 'bk': jax.random.normal(ks[6], (DIM,), jnp.float32) * s, 'wv': jax.random.normal(ks[7], (DIM, DIM), jnp.float32) * s, 'bv': jax.random.normal(ks[8], (DIM,), jnp.float32) * s, 'wo': jax.random.normal(ks[9], (DIM, DIM), jnp.float32) * s, 'bo': jax.random.normal(ks[10], (DIM,), jnp.float32) * s}
    _L0_xattn_all = _L0_xattn_setup()
    _L0_xattn_in = {k: v for k, v in _L0_xattn_all.items() if k in ('wq', 'bq', 'wk', 'bk', 'wv', 'bv', 'wo', 'bo')}
    del _L0_xattn_all

    def _L0_ffn_setup():
        import jax, jax.numpy as jnp
        import numpy as np
        E = 32
        H = 128
        I = 64
        G = 8
        TKG = 4
        TOPK = 8
        NSH = 2
        SCALE = 2.5
        key = jax.random.key(seed)
        ks = jax.random.split(key, 10)
        s = 0.02
        return {'hidden_states': jax.random.normal(ks[0], (2, 128, H), jnp.float32), 'gate_w': jax.random.normal(ks[1], (E, H), jnp.float32) * s, 'gate_bias': jax.random.normal(ks[2], (E,), jnp.float32) * s, 'w_gate': jax.random.normal(ks[3], (E, I, H), jnp.float32) * s, 'w_up': jax.random.normal(ks[4], (E, I, H), jnp.float32) * s, 'w_down': jax.random.normal(ks[5], (E, H, I), jnp.float32) * s, 'sh_gate': jax.random.normal(ks[6], (I * NSH, H), jnp.float32) * s, 'sh_up': jax.random.normal(ks[7], (I * NSH, H), jnp.float32) * s, 'sh_down': jax.random.normal(ks[8], (H, I * NSH), jnp.float32) * s}
    _L0_ffn_all = _L0_ffn_setup()
    _L0_ffn_in = {k: v for k, v in _L0_ffn_all.items() if k in ('gate_w', 'gate_bias', 'w_gate', 'w_up', 'w_down', 'sh_gate', 'sh_up', 'sh_down')}
    del _L0_ffn_all
    return {'x': x, 'ctx_1024': ctx_1024, 'L0_xattn_wq': _L0_xattn_in['wq'], 'L0_xattn_bq': _L0_xattn_in['bq'], 'L0_xattn_wk': _L0_xattn_in['wk'], 'L0_xattn_bk': _L0_xattn_in['bk'], 'L0_xattn_wv': _L0_xattn_in['wv'], 'L0_xattn_bv': _L0_xattn_in['bv'], 'L0_xattn_wo': _L0_xattn_in['wo'], 'L0_xattn_bo': _L0_xattn_in['bo'], 'L0_ffn_gate_w': _L0_ffn_in['gate_w'], 'L0_ffn_gate_bias': _L0_ffn_in['gate_bias'], 'L0_ffn_w_gate': _L0_ffn_in['w_gate'], 'L0_ffn_w_up': _L0_ffn_in['w_up'], 'L0_ffn_w_down': _L0_ffn_in['w_down'], 'L0_ffn_sh_gate': _L0_ffn_in['sh_gate'], 'L0_ffn_sh_up': _L0_ffn_in['sh_up'], 'L0_ffn_sh_down': _L0_ffn_in['sh_down']}

def reference(x, ctx_1024, L0_xattn_wq, L0_xattn_bq, L0_xattn_wk, L0_xattn_bk, L0_xattn_wv, L0_xattn_bv, L0_xattn_wo, L0_xattn_bo, L0_ffn_gate_w, L0_ffn_gate_bias, L0_ffn_w_gate, L0_ffn_w_up, L0_ffn_w_down, L0_ffn_sh_gate, L0_ffn_sh_up, L0_ffn_sh_down):
    import jax
    import jax.numpy as jnp

    def _L0_xattn_ref(query, key, value, wq, bq, wk, bk, wv, bv, wo, bo):
        import jax, jax.numpy as jnp
        import numpy as np
        DIM = 128
        NUM_HEAD = 16
        DIM_HEAD = DIM // NUM_HEAD
        B, S, _ = query.shape

        def proj(x, w, b):
            y = x @ w.T + b
            return y.reshape(B, -1, NUM_HEAD, DIM_HEAD).transpose(0, 2, 1, 3)
        Q = proj(query, wq, bq).astype(jnp.float32)
        K = proj(key, wk, bk).astype(jnp.float32)
        V = proj(value, wv, bv).astype(jnp.float32)
        energy = jnp.einsum('bhqd,bhkd->bhqk', Q, K) / np.sqrt(DIM_HEAD).astype(np.float32)
        attn = jax.nn.softmax(energy, axis=-1)
        out = jnp.einsum('bhqk,bhkd->bhqd', attn, V)
        out = out.transpose(0, 2, 1, 3).reshape(B, S, DIM)
        return out @ wo.T + bo

    def _L0_ffn_ref(hidden_states, gate_w, gate_bias, w_gate, w_up, w_down, sh_gate, sh_up, sh_down):
        import jax, jax.numpy as jnp
        import numpy as np
        E = 32
        H = 128
        I = 64
        G = 8
        TKG = 4
        TOPK = 8
        NSH = 2
        SCALE = 2.5
        B, S, Hd = hidden_states.shape
        h = hidden_states.reshape(-1, Hd)
        logits = h.astype(jnp.float32) @ gate_w.T
        scores = jax.nn.sigmoid(logits)
        sc = scores + gate_bias
        grp = sc.reshape(-1, G, E // G)
        group_scores = jax.lax.top_k(grp, 2)[0].sum(-1)
        gidx = jax.lax.top_k(group_scores, TKG)[1]
        gmask = jnp.sum(jax.nn.one_hot(gidx, G, dtype=sc.dtype), axis=1)
        smask = jnp.repeat(gmask, E // G, axis=1)
        masked = jnp.where(smask > 0, sc, jnp.zeros_like(sc))
        tki = jax.lax.top_k(masked, TOPK)[1]
        tkw = jnp.take_along_axis(scores, tki, axis=1)
        tkw = tkw / (tkw.sum(-1, keepdims=True) + 1e-20)
        tkw = tkw * SCALE
        combine = (jax.nn.one_hot(tki, E, dtype=tkw.dtype) * tkw[..., None]).sum(1)
        g = jax.nn.silu(jnp.einsum('th,eih->tei', h, w_gate))
        u = jnp.einsum('th,eih->tei', h, w_up)
        routed = jnp.einsum('tei,ehi->th', g * u * combine[:, :, None], w_down)
        sg = jax.nn.silu(h @ sh_gate.T)
        shared = sg * (h @ sh_up.T) @ sh_down.T
        return (routed + shared).reshape(B, S, Hd)
    x = x + _L0_xattn_ref(_layernorm(x, axis=-1), ctx_1024, ctx_1024, L0_xattn_wq, L0_xattn_bq, L0_xattn_wk, L0_xattn_bk, L0_xattn_wv, L0_xattn_bv, L0_xattn_wo, L0_xattn_bo)
    x = x + _L0_ffn_ref(_layernorm(x, axis=-1), L0_ffn_gate_w, L0_ffn_gate_bias, L0_ffn_w_gate, L0_ffn_w_up, L0_ffn_w_down, L0_ffn_sh_gate, L0_ffn_sh_up, L0_ffn_sh_down)
    return x

_drawn_inputs = setup_inputs


def setup_inputs(seed=0):
    import zlib

    import numpy as np

    out = dict(_drawn_inputs(seed))
    spreads = {}
    factors = {'L0_xattn_bq': 3.131,
     'L0_xattn_bk': 8.0,
     'L0_ffn_gate_w': 8.0,
     'L0_ffn_gate_bias': 8.0,
     'L0_ffn_w_gate': 8.0,
     'L0_ffn_w_up': 8.0,
     'L0_ffn_w_down': 8.0,
     'L0_ffn_sh_gate': 8.0,
     'L0_ffn_sh_up': 8.0,
     'L0_ffn_sh_down': 8.0}
    for name, (base, spread) in spreads.items():
        noise = np.random.default_rng([zlib.crc32(name.encode()), seed]).standard_normal(out[name].shape)
        drawn = base * np.exp(spread * noise) if base else spread * noise
        out[name] = jnp.asarray(drawn.astype(out[name].dtype))
    for name, factor in factors.items():
        out[name] = (out[name] * factor).astype(out[name].dtype)
    return out
```

```python
from contextlib import ExitStack

import numpy as np

import concourse.bass as bass
from concourse import mybir

F32 = mybir.dt.float32
BF16 = mybir.dt.bfloat16
ALU = mybir.AluOpType
ACT = mybir.ActivationFunctionType
AX = mybir.AxisListType

P = 128
B, SQ, D = 16, 256, 128
SK = 1601
NH, DH = 16, 8
QB = SQ // P
NC = (SK + P - 1) // P
LAST = SK - (NC - 1) * P
PAIRS = NH // 2
NPAIR = B * PAIRS
COPIES_K = (0, 0, 0, 1, 1, 2)
COPIES_Q = (0, 1, 2, 0, 1, 0)
NCOPY = len(COPIES_K)
ROWS = NCOPY * DH
VW = 32
NE, NI, TOPK, TOPG, NG = 32, 64, 8, 4, 8
EPJ = P // NI
UNITS = NE // EPJ
TB = 512
TT = TB // P
NBLK = B * SQ // TB
EPS = 1e-5
SCALE = 2.5
QSCALE = float(1.0 / np.sqrt(np.float32(DH)))
BANK = 512
REPLACED = -3.3e38
UNMATCHED = -3.0e38
SLOTS = 4
HALVES = ((0, 801), (801, 800))


class Steps:

    def __init__(self, eng, sem, base=0):
        self.eng, self.sem, self.base, self.n = eng, sem, base, 0

    def mark(self, ins):
        ins.then_inc(self.sem, 1)
        self.n += 1

    def wait(self):
        self.eng.wait_ge(self.sem, self.base + self.n)

    def wait_apart(self, passed):
        self.wait()
        self.eng.sem_inc(passed, 1)


def project(nc, io, ke, qe, ve):
    with ExitStack() as ctx:
        sb = lambda name, shape, dt=F32: ctx.enter_context(nc.sbuf_tensor(name, shape, dt))
        sem = lambda name: ctx.enter_context(nc.semaphore(name))
        two = lambda name: [sem(f"{name}{s}") for s in range(2)]

        wq, wk, wv = sb("wq", [P, D]), sb("wk", [P, D]), sb("wv", [P, D])
        bqk = sb("bqk", [P, 3])
        bv = sb("bv", [P, D])
        ident = sb("ident1", [P, P])
        eps = sb("eps1", [P, 1])
        ctxt = sb("ctxt", [P, 2, SK])
        xin = sb("xin", [P, 2, QB, D])
        kf, kr = sb("kf", [P, 2, SK]), sb("kr", [P, 2, SK])
        kp = sb("kp", [P, 2, 3, SK], BF16)
        qf, qr = sb("qf", [P, 2, SQ]), sb("qr", [P, 2, SQ])
        qp = sb("qp", [P, 2, 3, SQ], BF16)
        vs = sb("vs", [P, 2, PAIRS, NC, VW])
        st, mv = sb("st", [P, 2, QB, 6]), sb("mv", [P, 2, QB, 2])
        rs = sb("rs", [P, 2, QB])
        xn, xt = sb("xn", [P, 2, QB, D]), sb("xt", [P, 2, SQ])
        ps = ctx.enter_context(nc.psum_tensor("ps1", [P, 8 * BANK], F32))
        k_ps = ps[:, 0:SK]
        v_ps = [ps[:, (4 + n) * BANK:(5 + n) * BANK].rearrange("p (c n) -> p c n", c=4) for n in range(2)]
        q_ps = ps[:, 6 * BANK:6 * BANK + SQ]
        t_ps = ps[:, 7 * BANK:7 * BANK + SQ]

        const_in = sem("const_in")
        const_ready = sem("const_ready")
        ctx_in, x_in = two("ctx_in"), two("x_in")
        kv_projected = two("kv_projected")
        k_done, k_evacuated = sem("k_done"), sem("k_evacuated")
        v_group, v_evacuated = sem("v_group"), sem("v_evacuated")
        kf_ready, k_high = two("kf_ready"), two("k_high")
        k_split, q_split = two("k_split"), two("q_split")
        var_ready, std_ready = sem("var_ready"), sem("std_ready")
        x_normed, x_turned, xt_ready = sem("x_normed"), sem("x_turned"), sem("xt_ready")
        q_done, q_ready = sem("q_done"), sem("q_ready")
        stored = two("stored")
        dve_step, passed = sem("dve_step1"), sem("passed1")
        block = ctx.enter_context(nc.Block())
        GROUPS = [range(g, min(g + 4, NC)) for g in range(0, NC, 4)]
        NG4 = len(GROUPS)

        @block.gpsimd
        def _(pool):
            for s in range(2):
                nc.gpsimd.memset(vs[:, s], 0.0).then_inc(const_ready, 1)
            pool.wait_ge(const_ready, 2)
            for s in range(2):
                for h in range(2):
                    nc.gpsimd.memset(vs[:, s, :, :, 9 * h + 8:9 * h + 9], 1.0).then_inc(const_ready, 1)
            nc.gpsimd.memset(eps[:], EPS).then_inc(const_ready, 1)
            with pool.Fori(0, B // 2) as i:
                for s in range(2):
                    b = 2 * i + s
                    pool.wait_ge(kv_projected[s], i)
                    pool.dma_start(ctxt[:, s], io["ctxT"][bass.ds(b, 1)].rearrange("a c k -> (a c) k")).then_inc(ctx_in[s], 16)
                    pool.wait_ge(x_normed, 2 * i)
                    pool.dma_start(xin[:, s], io["x"][bass.ds(b, 1)].rearrange("a (t p) d -> p (a t) d", p=P)).then_inc(x_in[s], 16)

        @block.sync
        def _(sp):
            for t, name in ((wq, "wqT"), (wk, "wkT"), (wv, "wvT"), (ident, "ident")):
                sp.dma_start(t[:], io[name]).then_inc(const_in, 16)
            sp.dma_start(bqk[:, 0:1], io["bq"].rearrange("(d a) -> d a", a=1)).then_inc(const_in, 16)
            sp.dma_start(bqk[:, 1:2], io["bk"].rearrange("(d a) -> d a", a=1)).then_inc(const_in, 16)
            sp.dma_start(bv[:], io["bv"].partition_broadcast(P)).then_inc(const_in, 16)
            with sp.Fori(0, B // 2) as i:
                for s in range(2):
                    b = 2 * i + s
                    sp.wait_ge(q_split[s], i + 1)
                    for c, part in enumerate(COPIES_Q):
                        sp.dma_start(qe[bass.ds(b, 1), :, c].rearrange("a r q -> (a r) q"), qp[:, s, part]).then_inc(stored[s], 16)
                    sp.wait_ge(v_evacuated, NG4 * (b + 1) + 1)
                    sp.dma_start(ve[bass.ds(b, 1)].rearrange("a n p w -> p (a n) w"),
                                 vs[:, s].rearrange("p n c w -> p n (c w)")).then_inc(stored[s], 16)
                    sp.wait_ge(k_split[s], i + 1)
                    for c, part in enumerate(COPIES_K):
                        sp.dma_start(ke[bass.ds(b, 1), :, c].rearrange("a r k -> (a r) k"), kp[:, s, part]).then_inc(stored[s], 16)
            for s in range(2):
                sp.wait_ge(stored[s], 16 * (2 * NCOPY + 1) * B // 2)

        @block.tensor
        def _(pe):
            pe.wait_ge(const_in, 7 * 16)
            with pe.Fori(0, B // 2) as i:
                for s in range(2):
                    n = 2 * i + s
                    pe.wait_ge(ctx_in[s], 16 * (i + 1))
                    pe.wait_ge(k_evacuated, n)
                    for a in range(0, SK, BANK):
                        w = min(BANK, SK - a)
                        last = nc.tensor.matmul(k_ps[:, a:a + w], wk[:], ctxt[:, s, a:a + w], start=True, stop=True)
                    last.then_inc(k_done, 1)
                    pe.wait_ge(x_normed, n + 1)
                    for t in range(QB):
                        last = nc.tensor.transpose(t_ps[:, t * P:(t + 1) * P], xn[:, s, t], ident[:])
                    last.then_inc(x_turned, 1)
                    for g, chunks in enumerate(GROUPS):
                        pe.wait_ge(v_evacuated, NG4 * n + g)
                        for c in chunks:
                            w = min(P, SK - c * P)
                            last = nc.tensor.matmul(v_ps[g % 2][0:w, c % 4], ctxt[:, s, c * P:c * P + w], wv[:], start=True, stop=True)
                        if g == NG4 - 1:
                            last.then_inc(kv_projected[s], 1)
                        else:
                            last.then_inc(v_group, 1)
                        if g == 1:
                            pe.wait_ge(xt_ready, n + 1)
                            pe.wait_ge(q_ready, n)
                            nc.tensor.matmul(q_ps, wq[:], xt[:, s], start=True, stop=True).then_inc(q_done, 1)

        @block.scalar
        def _(act):
            act.wait_ge(const_in, 7 * 16)
            act.wait_ge(const_ready, 7)
            act.sem_inc(v_evacuated, 1)
            nc.scalar.mul(bqk[:, 2:3], bqk[:, 0:1], QSCALE).then_inc(const_ready, 1)
            act.wait_ge(const_ready, 8)
            with act.Fori(0, B // 2) as i:
                for s in range(2):
                    n = 2 * i + s
                    act.wait_ge(var_ready, n + 1)
                    nc.scalar.activation(rs[:, s], mv[:, s, :, 1], ACT.Sqrt, bias=eps[:]).then_inc(std_ready, 1)
                    act.wait_ge(k_done, n + 1)
                    act.wait_ge(k_split[s], i)
                    nc.scalar.activation(kf[:, s], k_ps, ACT.Identity, bias=bqk[:, 1:2]).then_inc(kf_ready[s], 1)
                    act.wait_ge(stored[s], 16 * (2 * NCOPY + 1) * i)
                    nc.scalar.activation(kp[:, s, 0], k_ps, ACT.Identity, bias=bqk[:, 1:2]).then_inc(k_evacuated, 1)
                    act.wait_ge(x_turned, n + 1)
                    nc.scalar.copy(xt[:, s], t_ps).then_inc(xt_ready, 1)
                    act.wait_ge(q_done, n + 1)
                    nc.scalar.activation(qf[:, s], q_ps, ACT.Identity, bias=bqk[:, 2:3], scale=QSCALE).then_inc(q_ready, 1)

        @block.vector
        def _(dve):
            dve.wait_ge(const_in, 7 * 16)
            dve.wait_ge(const_ready, 8)
            per = 2 * (QB + QB + 1 + 2 + 3 - 1)
            with dve.Fori(0, B // 2) as i:
                step = Steps(dve, dve_step, per * i)
                for s in range(2):
                    n = 2 * i + s
                    dve.wait_ge(x_in[s], 16 * (i + 1))
                    for t in range(QB):
                        step.mark(nc.vector.bn_stats(st[:, s, t], xin[:, s, t]))
                    step.wait_apart(passed)
                    for t in range(QB - 1):
                        step.mark(nc.vector.bn_aggr(mv[:, s, t], st[:, s, t]))
                    step.wait_apart(passed)
                    nc.vector.bn_aggr(mv[:, s, QB - 1], st[:, s, QB - 1]).then_inc(var_ready, 1)
                    dve.wait_ge(std_ready, n + 1)
                    step.mark(nc.vector.reciprocal(rs[:, s], rs[:, s]))
                    step.wait()
                    for t in range(QB):
                        last = nc.vector.tensor_scalar(xn[:, s, t], xin[:, s, t], mv[:, s, t, 0:1], rs[:, s, t:t + 1], ALU.subtract, ALU.mult)
                    last.then_inc(x_normed, 1)
                    dve.wait_ge(k_evacuated, n + 1)
                    step.mark(nc.vector.tensor_tensor(kr[:, s], kf[:, s], kp[:, s, 0], ALU.subtract))
                    step.wait()
                    step.mark(nc.vector.tensor_copy(kp[:, s, 1], kr[:, s]))
                    step.wait()
                    nc.vector.tensor_tensor(kp[:, s, 2], kr[:, s], kp[:, s, 1], ALU.subtract).then_inc(k_split[s], 1)
                    for g, chunks in enumerate(GROUPS):
                        if g == NG4 - 1:
                            dve.wait_ge(kv_projected[s], i + 1)
                        else:
                            dve.wait_ge(v_group, (NG4 - 1) * n + g + 1)
                        w = P if g < NG4 - 1 else LAST
                        for h in range(2):
                            out = vs[0:w, s, :, chunks[0]:chunks[-1] + 1, 9 * h:9 * h + DH].rearrange("p n c d -> p c n d")
                            src = v_ps[g % 2][0:w, 0:len(chunks)].rearrange("p c (n h d) -> p c n h d", h=2, d=DH)[:, :, :, h]
                            bias = bv[0:w].rearrange("p (n h d) -> p n h d", h=2, d=DH)[:, :, h].unsqueeze(1).broadcast_to([w, len(chunks), PAIRS, DH])
                            ins = nc.vector.tensor_tensor(out, src, bias, ALU.add)
                        ins.then_inc(v_evacuated, 1)
                    dve.wait_ge(q_ready, n + 1)
                    step.mark(nc.vector.tensor_copy(qp[:, s, 0], qf[:, s]))
                    step.wait()
                    step.mark(nc.vector.tensor_tensor(qr[:, s], qf[:, s], qp[:, s, 0], ALU.subtract))
                    step.wait()
                    step.mark(nc.vector.tensor_copy(qp[:, s, 1], qr[:, s]))
                    step.wait()
                    nc.vector.tensor_tensor(qp[:, s, 2], qr[:, s], qp[:, s, 1], ALU.subtract).then_inc(q_split[s], 1)


def attend(nc, io, ke, qe, ve, att):
    with ExitStack() as ctx:
        sb = lambda name, shape, dt=F32: ctx.enter_context(nc.sbuf_tensor(name, shape, dt))
        sem = lambda name: ctx.enter_context(nc.semaphore(name))
        slots = lambda name: [sem(f"{name}{s}") for s in range(SLOTS)]

        ident = sb("ident2", [P, P])
        identb = sb("identb2", [P, P], BF16)
        pick = sb("pick", [P, 2 * (DH + 1)])
        kx = [sb(f"kx{s}", [P, SK], BF16) for s in range(SLOTS)]
        qx = [sb(f"qx{s}", [P, 2 * SQ], BF16) for s in range(SLOTS)]
        qm = [sb(f"qm{s}", [P, 2 * SQ], BF16) for s in range(SLOTS)]
        vx = [sb(f"vx{s}", [P, NC * VW]) for s in range(SLOTS)]
        prob = [sb(f"prob{s}", [P, NC, 2 * SQ]) for s in range(2)]
        half_max = sb("half_max", [P, 2, 4, 2])
        neg, neg_rest = sb("neg", [P, 2, 4]), sb("neg_rest", [P, 2, 4])
        neg_parts = sb("neg_parts", [P, 2, 4, 3], BF16)
        neg_rows = [sb(f"neg_rows{s}", [3, 4 * P], BF16) for s in range(2)]
        ev = [sb(f"ev{s}", [P, 2 * SQ]) for s in range(2)]
        rsum = sb("rsum", [P, 2, 4])
        ps = ctx.enter_context(nc.psum_tensor("ps2", [P, 8 * BANK], F32))
        s_ps = [ps[:, n * BANK:(n + 1) * BANK] for n in range(2)]
        m_ps = [ps[:, (2 + 2 * n) * BANK:(4 + 2 * n) * BANK] for n in range(2)]
        o_ps = ps[:, 6 * BANK:7 * BANK]
        w_ps = ps[:, 7 * BANK:7 * BANK + 4 * (DH + 1)]
        t_ps = ps[:, 7 * BANK + 128:7 * BANK + 128 + 4 * P // 2].bitcast(BF16)[0:3]

        const_in, const_ready = sem("const_in2"), sem("const_ready2")
        loaded, pair_done, neg_stored = slots("loaded"), slots("pair_done"), slots("neg_stored")
        max_scored, max_reduced = sem("max_scored"), sem("max_reduced")
        neg_ready, neg_split = sem("neg_ready"), sem("neg_split")
        neg_turned, neg_copied = sem("neg_turned"), sem("neg_copied")
        scored, exped = sem("scored"), sem("exped")
        evacuated, picked, normalised = sem("evacuated"), sem("picked"), sem("normalised")
        pool_step, dve_step, passed = sem("pool_step2"), sem("dve_step2"), sem("passed2")
        block = ctx.enter_context(nc.Block())

        def of(i, t):
            return SLOTS * i + t, t % SLOTS, i + t // SLOTS

        @block.gpsimd
        def _(pool):
            for s in range(SLOTS):
                nc.gpsimd.memset(kx[s][:], 1.0).then_inc(const_ready, 1)
                nc.gpsimd.memset(qx[s][:], 0.0).then_inc(const_ready, 1)
                nc.gpsimd.memset(qm[s][:], 0.0).then_inc(const_ready, 1)
            nc.gpsimd.memset(ev[1][:], 1.0).then_inc(const_ready, 1)
            pool.wait_ge(const_in, 32)
            nc.gpsimd.tensor_copy(identb[:], ident[:]).then_inc(const_ready, 1)

            def split(i, t, step):
                n, _, _ = of(i, t)
                a = t % 2
                whole, rest = neg[:, a], neg_rest[:, a]
                pool.wait_ge(neg_ready, n + 1)
                pool.sem_inc(passed, 1)
                step.mark(nc.gpsimd.tensor_copy(neg_parts[:, a, :, 0], whole))
                step.wait()
                step.mark(nc.gpsimd.tensor_tensor(rest, whole, neg_parts[:, a, :, 0], ALU.subtract))
                step.wait_apart(passed)
                step.mark(nc.gpsimd.tensor_copy(neg_parts[:, a, :, 1], rest))
                step.wait()
                nc.gpsimd.tensor_tensor(neg_parts[:, a, :, 2], rest, neg_parts[:, a, :, 1], ALU.subtract).then_inc(neg_split, 1)

            first = Steps(pool, pool_step)
            split(0, 0, first)
            split(0, 1, first)
            with pool.Fori(0, NPAIR // SLOTS - 1) as i:
                step = Steps(pool, pool_step, 6 + 3 * SLOTS * i)
                for t in range(SLOTS):
                    split(i, t + 2, step)
            i = NPAIR // SLOTS - 1
            step = Steps(pool, pool_step, 6 + 3 * SLOTS * i)
            for t in range(SLOTS - 2):
                split(i, t + 2, step)

        @block.sync
        def _(sp):
            sp.dma_start(ident[:], io["ident"]).then_inc(const_in, 16)
            sp.dma_start(pick[:], io["pick"]).then_inc(const_in, 16)
            sp.wait_ge(const_ready, 3 * SLOTS)
            kep = ke.rearrange("b (n h r) c k -> (b n) h (r c) k", h=2, r=DH)
            qep = qe.rearrange("b (n h r) c q -> (b n) h (r c) q", h=2, r=DH)
            vep = ve.rearrange("b n p w -> (b n) p w")

            def load(i, t):
                n, s, uses = of(i, t)
                at = bass.ds(n, 1)
                sp.wait_ge(pair_done[s], uses)
                for h in range(2):
                    rows, cols = slice(64 * h, 64 * h + ROWS), slice(SQ * h, SQ * h + SQ)
                    sp.dma_start(qm[s][rows, cols], qep[at, h].rearrange("a r q -> (a r) q")).then_inc(loaded[s], 16)
                    sp.dma_start(kx[s][rows, :], kep[at, h].rearrange("a r k -> (a r) k")).then_inc(loaded[s], 16)
                    sp.dma_start(qx[s][rows, cols], qep[at, h].rearrange("a r q -> (a r) q")).then_inc(loaded[s], 16)
                sp.dma_start(vx[s][:], vep[at].rearrange("a p w -> (a p) w")).then_inc(loaded[s], 16)

            def store_neg(i, t):
                n, s, uses = of(i, t)
                sp.wait_ge(neg_copied, n + 1)
                for h in range(2):
                    sp.dma_start(qx[s][64 * h + ROWS:64 * h + ROWS + 3, SQ * h:SQ * h + SQ],
                                 neg_rows[t % 2][:, SQ * h:SQ * h + SQ]).then_inc(neg_stored[s], 16)

            for t in range(3):
                load(0, t)
            store_neg(0, 0)
            with sp.Fori(0, NPAIR // SLOTS - 1) as i:
                for t in range(SLOTS):
                    load(i, t + 3)
                    store_neg(i, t + 1)
            i = NPAIR // SLOTS - 1
            load(i, 3)
            for t in range(SLOTS - 1):
                store_neg(i, t + 1)

        @block.tensor
        def _(pe):
            pe.wait_ge(const_in, 32)
            pe.wait_ge(const_ready, 3 * SLOTS + 2)

            def max_unit(i, t, u, first=False):
                n, s, uses = of(i, t)
                if u == 0:
                    pe.wait_ge(loaded[s], 16 * 7 * (uses + 1))
                if not (first and u < 2):
                    pe.wait_ge(max_reduced, 8 * n + u - 1)
                a, w = HALVES[u % 2]
                for o in range(0, w, BANK):
                    m = min(BANK, w - o)
                    last = nc.tensor.matmul(m_ps[u % 2][:, o:o + m], qm[s][:, (u // 2) * P:(u // 2 + 1) * P],
                                            kx[s][:, a + o:a + o + m], start=True, stop=True)
                last.then_inc(max_scored, 1)

            def turn_neg(i, t):
                n, _, _ = of(i, t)
                pe.wait_ge(neg_split, n + 1)
                for u in range(4):
                    last = nc.tensor.transpose(t_ps[:, u * P:(u + 1) * P], neg_parts[:, t % 2, u], identb[:])
                last.then_inc(neg_turned, 1)

            def score(i, t, c):
                n, s, uses = of(i, t)
                if c == 0:
                    pe.wait_ge(neg_stored[s], 16 * 2 * (uses + 1))
                pe.wait_ge(exped, NC * n + c)
                w = P if c < NC - 1 else LAST
                nc.tensor.matmul(s_ps[(NC * t + c) % 2][0:w, :], kx[s][:, c * P:c * P + w], qx[s][:, :], start=True, stop=True).then_inc(scored, 1)

            def weigh(i, t, c):
                n, s, uses = of(i, t)
                if c == 0:
                    pe.wait_ge(evacuated, n + 1)
                pe.wait_ge(exped, NC * n + c + 1 + 1)
                w = P if c < NC - 1 else LAST
                j = 32 * (c % 4)
                last = nc.tensor.matmul(o_ps[j:j + VW, :], vx[s][0:w, c * VW:(c + 1) * VW], prob[t % 2][0:w, c],
                                        start=c < 4, stop=c >= NC - 4)
                if c == NC - 1:
                    last.then_inc(pair_done[s], 1)

            def pick_out(i, t):
                n, _, _ = of(i, t)
                pe.wait_ge(evacuated, n + 1)
                pe.wait_ge(normalised, n)
                for u in range(4):
                    h = u // 2
                    last = nc.tensor.matmul(w_ps[:, u * (DH + 1):(u + 1) * (DH + 1)], ev[(t - 1) % 2][:, u * P:(u + 1) * P],
                                            pick[:, h * (DH + 1):(h + 1) * (DH + 1)], start=True, stop=True)
                last.then_inc(picked, 1)

            def pair(i, t, turn=True, ahead=True):
                n, _, _ = of(i, t)
                steps = [range(k, min(k + 2, NC)) for k in range(0, NC, 2)]
                for k, chunks in enumerate(steps):
                    for c in chunks:
                        score(i, t, c)
                    if k == 1 and turn:
                        pe.wait_ge(normalised, n)
                        turn_neg(i, t + 1)
                    if k == 3:
                        pe.wait_ge(neg_copied, n + 2 if turn else n + 1)
                        pick_out(i, t)
                    if ahead:
                        max_unit(i, t + 2, k)
                        if k == len(steps) - 1:
                            max_unit(i, t + 2, k + 1)
                    if k:
                        for c in steps[k - 1]:
                            weigh(i, t, c)
                for c in steps[-1]:
                    weigh(i, t, c)

            for t in range(2):
                for u in range(8):
                    max_unit(0, t, u, first=t == 0)
            turn_neg(0, 0)
            with pe.Fori(0, NPAIR // SLOTS - 1) as i:
                for t in range(SLOTS):
                    pair(i, t)
            i = NPAIR // SLOTS - 1
            for t in range(SLOTS):
                pair(i, t, turn=t + 1 < SLOTS, ahead=t + 2 < SLOTS)
            pick_out(i, SLOTS)

        @block.scalar
        def _(act):
            act.wait_ge(const_ready, 3 * SLOTS + 2)
            act.sem_inc(exped, 1)
            act.sem_inc(evacuated, 1)

            def copy_neg(i, t):
                n, _, _ = of(i, t)
                act.wait_ge(neg_turned, n + 1)
                nc.scalar.copy(neg_rows[t % 2][:], t_ps).then_inc(neg_copied, 1)

            def pair(i, t, turn=True):
                n, s, uses = of(i, t)
                for c in range(NC):
                    act.wait_ge(scored, NC * n + c + 1)
                    w = P if c < NC - 1 else LAST
                    nc.scalar.activation(prob[t % 2][0:w, c], s_ps[(NC * t + c) % 2][0:w, :], ACT.Exp).then_inc(exped, 1)
                    if c == 4 and turn:
                        copy_neg(i, t + 1)
                act.wait_ge(pair_done[s], uses + 1)
                nc.scalar.copy(ev[t % 2][:], o_ps).then_inc(evacuated, 1)

            copy_neg(0, 0)
            with act.Fori(0, NPAIR // SLOTS - 1) as i:
                for t in range(SLOTS):
                    pair(i, t)
            i = NPAIR // SLOTS - 1
            for t in range(SLOTS):
                pair(i, t, turn=t + 1 < SLOTS)

        @block.vector
        def _(dve):
            def reduce_unit(i, t, u):
                n, _, _ = of(i, t)
                dve.wait_ge(max_scored, 8 * n + u + 1)
                nc.vector.tensor_reduce(half_max[:, t % 2, u // 2, u % 2:u % 2 + 1], m_ps[u % 2][:, 0:HALVES[u % 2][1]],
                                        AX.X, ALU.max).then_inc(max_reduced, 1)

            def negate(i, t):
                n, _, _ = of(i, t)
                dve.wait_ge(max_reduced, 8 * (n + 1))
                nc.vector.tensor_reduce(neg[:, t % 2], half_max[:, t % 2], AX.X, ALU.max, negate=True).then_inc(neg_ready, 1)

            def normalise(i, t, step):
                n, _, _ = of(i, t)
                dve.wait_ge(picked, n + 1)
                out = w_ps.rearrange("p (u r) -> p u r", u=4)
                step.mark(nc.vector.reciprocal(rsum[:, t % 2].unsqueeze(2), out[:, :, DH:DH + 1]))
                step.wait()
                to = att[:, bass.ds(n, 1)].rearrange("p a b (h d) -> p (a h) b d", h=2)
                nc.vector.tensor_tensor(to, out[:, :, 0:DH].rearrange("p (h b) d -> p h b d", h=2),
                                        rsum[:, t % 2].rearrange("p (h b) -> p h b", h=2).unsqueeze(3).broadcast_to([P, 2, QB, DH]),
                                        ALU.mult).then_inc(normalised, 1)

            def pair(i, t, step, ahead=True):
                if ahead:
                    for u in range(5):
                        reduce_unit(i, t + 2, u)
                normalise(i, t, step)
                if ahead:
                    for u in range(5, 8):
                        reduce_unit(i, t + 2, u)
                    negate(i, t + 2)

            for t in range(2):
                for u in range(8):
                    reduce_unit(0, t, u)
                negate(0, t)
            with dve.Fori(0, NPAIR // SLOTS - 1) as i:
                step = Steps(dve, dve_step, SLOTS * i)
                for t in range(SLOTS):
                    pair(i, t, step)
            i = NPAIR // SLOTS - 1
            step = Steps(dve, dve_step, SLOTS * i)
            for t in range(SLOTS):
                pair(i, t, step, ahead=t + 2 < SLOTS)
            normalise(i, SLOTS, step)


def mix(nc, io, att, out):
    with ExitStack() as ctx:
        sb = lambda name, shape, dt=F32: ctx.enter_context(nc.sbuf_tensor(name, shape, dt))
        sem = lambda name: ctx.enter_context(nc.semaphore(name))

        ident = sb("ident3", [P, P])
        identb = sb("identb3", [P, P], BF16)
        wo, gw = sb("wo", [P, D]), sb("gw", [P, NE])
        bo, gb = sb("bo", [P, D]), sb("gb", [P, NE])
        eps = sb("eps3", [P, 1])
        wg, wu = sb("wg", [P, UNITS + 1, P]), sb("wu", [P, UNITS + 1, P])
        wd = sb("wd", [P, UNITS + 1, D])
        spread_f = sb("spread_f", [3 * NE, UNITS, P])
        spread = sb("spread", [3 * NE, UNITS, P], BF16)
        x1 = [sb(f"x1{s}", [P, TT, D]) for s in range(2)]
        ht = [sb(f"ht{s}", [P, TB]) for s in range(2)]
        ct = [sb(f"ct{s}", [3 * NE, TB], BF16) for s in range(2)]
        xin = sb("xin3", [P, TT, D])
        ob, ot = sb("ob", [P, TT, D]), sb("ot", [P, TB])
        st, mv, rs = sb("st3", [P, TT, 6]), sb("mv3", [P, TT, 2]), sb("rs3", [P, TT])
        hn = sb("hn", [P, TT, D])
        score = sb("score", [P, TT, NE])
        biased, masked, left = sb("biased", [P, TT, NE]), sb("masked", [P, TT, NE]), sb("left", [P, TT, NE])
        hi, lo = sb("hi", [P, TT * NG, 2]), sb("lo", [P, TT * NG, 2])
        top, second = sb("top", [P, TT * NG]), sb("second", [P, TT * NG])
        gscore, gleft = sb("gscore", [P, TT, NG]), sb("gleft", [P, TT, NG])
        best = sb("best", [P, TT, 8])
        total = sb("total", [P, TT])
        cw, cr = sb("cw", [P, TT, NE]), sb("cr", [P, TT, NE])
        cp = sb("cp", [P, TT, 3, NE], BF16)
        sg = [sb(f"sg{n}", [P, TB]) for n in range(2)]
        gu = [sb(f"gu{n}", [P, TB]) for n in range(2)]
        hid = [sb(f"hid{n}", [P, TB]) for n in range(2)]
        y = sb("y", [P, TT, D])
        ps = ctx.enter_context(nc.psum_tensor("ps3", [P, 8 * BANK], F32))
        bank = lambda n: ps[:, n * BANK:(n + 1) * BANK]
        g_ps, u_ps, c_ps = [bank(0), bank(1)], [bank(2), bank(3)], [bank(4), bank(5)]
        y_ps = bank(6).rearrange("p (t d) -> p t d", t=TT)
        z_ps = bank(7)
        z_tiles = z_ps.rearrange("p (t d) -> p t d", t=TT)
        z_bf = z_ps.bitcast(BF16)[0:3 * NE, 0:TB]

        const_in, const_ready = sem("const_in3"), sem("const_ready3")
        x_in, ob_ready = sem("x_in3"), sem("ob_ready")
        pe_stage, act_stage, dve_stage = sem("pe_stage"), sem("act_stage"), sem("dve_stage")
        gated, up, spreaded = sem("gated"), sem("up"), sem("spreaded")
        silued, multiplied, hidden = sem("silued"), sem("multiplied"), sem("hidden")
        y_done, y_ready, y_stored = sem("y_done"), sem("y_ready"), sem("y_stored")
        dve_step, passed, gathers = sem("dve_step3"), sem("passed3"), sem("gathers")
        block = ctx.enter_context(nc.Block())
        ALL = UNITS + 1
        PE_ST, ACT_ST, DVE_ST = 5, 5, 4
        CONSTS = 12
        STEPS = 44

        def blocks(eng, prepare, expert_block):
            for k in range(ALL):
                prepare(0, 0, k)
            with eng.Fori(0, NBLK // 2 - 1) as i:
                for s in range(2):
                    expert_block(2 * i + s, s, lambda k: prepare(2 * i + s + 1, 1 - s, k))
            expert_block(NBLK - 2, 0, lambda k: prepare(NBLK - 1, 1, k))
            expert_block(NBLK - 1, 1, lambda k: None)

        @block.gpsimd
        def _(pool):
            nc.gpsimd.memset(eps[:], EPS).then_inc(const_ready, 1)
            pool.wait_ge(const_in, 16 * CONSTS)
            nc.gpsimd.tensor_copy(identb[:], ident[:]).then_inc(const_ready, 1)
            nc.gpsimd.tensor_copy(spread[:], spread_f[:]).then_inc(const_ready, 1)

            def gather(n):
                for b2 in range(TT // QB):
                    src = att[:, bass.ds(1 + n * (PAIRS * TT // QB) + b2 * PAIRS, PAIRS)].rearrange("p a b c -> p b a c")
                    ins = nc.gpsimd.tensor_copy(ob[:, b2 * QB:(b2 + 1) * QB].rearrange("p b (a c) -> p b a c", a=PAIRS), src)
                ins.then_inc(ob_ready, 1)

            gather(0)
            with pool.Fori(1, NBLK) as n:
                pool.wait_ge(pe_stage, PE_ST * n - PE_ST + 1)
                pool.sem_inc(gathers, 1)
                gather(n)

        @block.sync
        def _(sp):
            xt = io["x"].rearrange("b (t p) d -> p (b t) d", p=P)
            ot_ = out.rearrange("b (t p) d -> p (b t) d", p=P)
            for t, name in ((ident, "ident"), (wo, "woT"), (gw, "gate_wT"), (spread_f, "spread")):
                sp.dma_start(t[:], io[name]).then_inc(const_in, 16)
            sp.dma_start(bo[:], io["bo"].partition_broadcast(P)).then_inc(const_in, 16)
            sp.dma_start(gb[:], io["gate_bias"].partition_broadcast(P)).then_inc(const_in, 16)
            sp.dma_start(xin[:], xt[:, 0:TT]).then_inc(x_in, 16)
            for t, name, shared in ((wg, "w_gateT", "sh_gateT"), (wu, "w_upT", "sh_upT"), (wd, "w_downT", "sh_downT")):
                sp.dma_start(t[:, 0:UNITS], io[name].rearrange("p (j n) -> p j n", n=P)).then_inc(const_in, 16)
                sp.dma_start(t[:, UNITS], io[shared]).then_inc(const_in, 16)

            def store(n):
                sp.wait_ge(y_ready, n + 1)
                sp.dma_start(ot_[:, bass.ds(TT * n, TT)], y[:]).then_inc(y_stored, 16)

            with sp.Fori(0, NBLK - 1) as n:
                sp.wait_ge(dve_stage, DVE_ST * n + 1)
                sp.dma_start(xin[:], xt[:, bass.ds(TT * n + TT, TT)]).then_inc(x_in, 16)
                store(n)
            store(NBLK - 1)
            sp.wait_ge(y_stored, 16 * NBLK)

        @block.tensor
        def _(pe):
            pe.wait_ge(const_in, 16 * CONSTS)
            pe.wait_ge(const_ready, 3)

            def prepare(n, s, k):
                if k == 0:
                    pe.wait_ge(ob_ready, n + 1)
                    for t in range(TT):
                        last = nc.tensor.transpose(z_tiles[:, t], ob[:, t], ident[:])
                elif k == 2:
                    pe.wait_ge(act_stage, ACT_ST * n + 1)
                    for t in range(TT):
                        last = nc.tensor.matmul(z_tiles[:, t], ot[:, t * P:(t + 1) * P], wo[:], start=True, stop=True)
                elif k == 7:
                    pe.wait_ge(dve_stage, DVE_ST * n + 3)
                    for t in range(TT):
                        last = nc.tensor.transpose(z_tiles[:, t], hn[:, t], ident[:])
                elif k == 9:
                    pe.wait_ge(act_stage, ACT_ST * n + 3)
                    for t in range(TT):
                        last = nc.tensor.matmul(z_ps[:, t * NE:(t + 1) * NE], ht[s][:, t * P:(t + 1) * P], gw[:], start=True, stop=True)
                elif k == 14:
                    pe.wait_ge(dve_stage, DVE_ST * n + 4)
                    for t in range(TT):
                        last = nc.tensor.transpose(z_bf[:, t * P:(t + 1) * P], cp[:, t].rearrange("p c e -> p (c e)"), identb[:])
                else:
                    return
                last.then_inc(pe_stage, 1)

            def down(n, j):
                if j == 0:
                    pe.wait_ge(y_ready, n)
                if j < UNITS:
                    pe.wait_ge(hidden, UNITS * n + j + 2)
                else:
                    pe.wait_ge(multiplied, ALL * n + j + 2)
                act_in = hid[j % 2] if j < UNITS else gu[j % 2]
                for t in range(TT):
                    last = nc.tensor.matmul(y_ps[:, t], act_in[:, t * P:(t + 1) * P], wd[:, j],
                                            start=j == 0 and t == 0, stop=j == ALL - 1, skip_group_check=True)
                if j == ALL - 1:
                    last.then_inc(y_done, 1)

            def expert_block(n, s, stage):
                for j in range(ALL):
                    if j == 0:
                        pe.wait_ge(act_stage, ACT_ST * (n + 1))
                    a, m = j % 2, ALL * n + j
                    free = m + (j == 0)
                    pe.wait_ge(silued, free)
                    nc.tensor.matmul(g_ps[a], wg[:, j], ht[s][:], start=True, stop=True).then_inc(gated, 1)
                    pe.wait_ge(multiplied, free)
                    nc.tensor.matmul(u_ps[a], wu[:, j], ht[s][:], start=True, stop=True).then_inc(up, 1)
                    if j < UNITS:
                        pe.wait_ge(hidden, UNITS * n + j)
                        nc.tensor.matmul(c_ps[a], spread[:, j], ct[s][:], start=True, stop=True).then_inc(spreaded, 1)
                    if j:
                        down(n, j - 1)
                    stage(j)
                down(n, ALL - 1)

            blocks(pe, prepare, expert_block)

        @block.scalar
        def _(act):
            act.wait_ge(const_ready, 3)

            def prepare(n, s, k):
                if k == 1:
                    act.wait_ge(pe_stage, PE_ST * n + 1)
                    ins = nc.scalar.copy(ot[:], z_ps)
                elif k == 5:
                    act.wait_ge(dve_stage, DVE_ST * n + 2)
                    ins = nc.scalar.activation(rs[:], mv[:, :, 1], ACT.Sqrt, bias=eps[:])
                elif k == 8:
                    act.wait_ge(pe_stage, PE_ST * n + 3)
                    ins = nc.scalar.copy(ht[s][:], z_ps)
                elif k == 10:
                    act.wait_ge(pe_stage, PE_ST * n + 4)
                    ins = nc.scalar.activation(score[:].rearrange("p t e -> p (t e)"), z_ps[:, 0:TT * NE], ACT.Exp, scale=-1.0)
                elif k == 15:
                    act.wait_ge(pe_stage, PE_ST * n + 5)
                    ins = nc.scalar.copy(ct[s][:], z_bf)
                else:
                    return
                ins.then_inc(act_stage, 1)

            def expert_block(n, s, stage):
                for j in range(ALL):
                    m = ALL * n + j
                    act.wait_ge(gated, m + 1)
                    act.wait_ge(multiplied, m + (j == 0))
                    nc.scalar.activation(sg[j % 2][:], g_ps[j % 2], ACT.Silu).then_inc(silued, 1)
                    stage(j)

            act.sem_inc(silued, 1)
            blocks(act, prepare, expert_block)

        @block.vector
        def _(dve):
            dve.wait_ge(const_in, 16 * CONSTS)

            step = Steps(dve, dve_step)

            def prepare(n, s, k):
                    flat = lambda t: t[:].rearrange("p t e -> p (t e)")
                    if k == 3:
                        step.base, step.n = STEPS * n, 0
                        dve.wait_ge(x_in, 16 * (n + 1))
                        dve.wait_ge(pe_stage, PE_ST * n + 2)
                        nc.vector.tensor_tensor(x1[s][:], z_tiles, xin[:], ALU.add).then_inc(dve_stage, 1)
                        dve.wait_ge(dve_stage, DVE_ST * n + 1)
                        step.mark(nc.vector.tensor_tensor(x1[s][:], x1[s][:], bo[:].unsqueeze(1).broadcast_to([P, TT, D]), ALU.add))
                    elif k == 4:
                        step.wait()
                        for t in range(TT):
                            step.mark(nc.vector.bn_stats(st[:, t], x1[s][:, t]))
                        step.wait_apart(passed)
                        for t in range(TT):
                            last = nc.vector.bn_aggr(mv[:, t], st[:, t])
                        last.then_inc(dve_stage, 1)
                    elif k == 6:
                        dve.wait_ge(act_stage, ACT_ST * n + 2)
                        step.mark(nc.vector.reciprocal(rs[:], rs[:]))
                        step.wait()
                        for t in range(TT):
                            last = nc.vector.tensor_scalar(hn[:, t], x1[s][:, t], mv[:, t, 0:1], rs[:, t:t + 1], ALU.subtract, ALU.mult)
                        last.then_inc(dve_stage, 1)
                    elif k == 11:
                        dve.wait_ge(act_stage, ACT_ST * n + 4)
                        step.mark(nc.vector.tensor_scalar(score[:], score[:], 1.0, None, ALU.add))
                        step.wait()
                        step.mark(nc.vector.reciprocal(score[:], score[:]))
                        step.wait()
                        step.mark(nc.vector.tensor_tensor(biased[:], score[:], gb[:].unsqueeze(1).broadcast_to([P, TT, NE]), ALU.add))
                        step.wait()
                        four = flat(biased).rearrange("p (g a b) -> p g a b", a=2, b=2)
                        step.mark(nc.vector.tensor_tensor(hi[:], four[:, :, :, 0], four[:, :, :, 1], ALU.max))
                        step.mark(nc.vector.tensor_tensor(lo[:], four[:, :, :, 0], four[:, :, :, 1], ALU.min))
                        step.wait()
                        step.mark(nc.vector.tensor_tensor(top[:], hi[:, :, 0], hi[:, :, 1], ALU.max))
                        step.mark(nc.vector.tensor_tensor(second[:], hi[:, :, 0], hi[:, :, 1], ALU.min))
                        step.mark(nc.vector.tensor_tensor(lo[:, :, 0], lo[:, :, 0], lo[:, :, 1], ALU.max))
                        step.wait()
                        step.mark(nc.vector.tensor_tensor(second[:], second[:], lo[:, :, 0], ALU.max))
                        step.wait()
                        step.mark(nc.vector.tensor_tensor(flat(gscore), top[:], second[:], ALU.add))
                    elif k == 12:
                        step.wait_apart(passed)
                        for t in range(TT):
                            step.mark(nc.vector.max(best[:, t], gscore[:, t]))
                        step.wait()
                        step.mark(nc.vector.memset(best[:, :, TOPG:8], UNMATCHED))
                        step.wait_apart(passed)
                        for t in range(TT):
                            step.mark(nc.vector.match_replace(gleft[:, t], best[:, t], gscore[:, t], REPLACED))
                        step.wait()
                        step.mark(nc.vector.tensor_tensor(gleft[:], gleft[:], gscore[:], ALU.is_lt))
                        step.wait()
                        step.mark(nc.vector.tensor_tensor(flat(masked).rearrange("p (g e) -> p g e", e=NE // NG),
                                                          flat(biased).rearrange("p (g e) -> p g e", e=NE // NG),
                                                          flat(gleft).unsqueeze(2).broadcast_to([P, TT * NG, NE // NG]), ALU.mult))
                        step.wait_apart(passed)
                        for t in range(TT):
                            step.mark(nc.vector.max(best[:, t], masked[:, t]))
                    elif k == 13:
                        step.wait_apart(passed)
                        for t in range(TT):
                            step.mark(nc.vector.match_replace(left[:, t], best[:, t], masked[:, t], REPLACED))
                        step.wait()
                        step.mark(nc.vector.tensor_tensor(left[:], left[:], masked[:], ALU.is_lt))
                        step.wait()
                        step.mark(nc.vector.tensor_tensor(cw[:], score[:], left[:], ALU.mult))
                        step.wait()
                        step.mark(nc.vector.tensor_reduce(total[:], cw[:], AX.X, ALU.add))
                        step.wait()
                        step.mark(nc.vector.tensor_scalar(total[:], total[:], 1e-20, None, ALU.add))
                        step.wait()
                        step.mark(nc.vector.reciprocal(total[:], total[:]))
                        step.wait()
                        step.mark(nc.vector.scalar_tensor_tensor(cw[:], cw[:], SCALE, total[:].unsqueeze(2).broadcast_to([P, TT, NE]), ALU.mult, ALU.mult))
                        step.wait()
                        step.mark(nc.vector.tensor_copy(cp[:, :, 0], cw[:]))
                        step.wait()
                        step.mark(nc.vector.tensor_tensor(cr[:], cw[:], cp[:, :, 0], ALU.subtract))
                        step.wait()
                        step.mark(nc.vector.tensor_copy(cp[:, :, 1], cr[:]))
                        step.wait()
                        nc.vector.tensor_tensor(cp[:, :, 2], cr[:], cp[:, :, 1], ALU.subtract).then_inc(dve_stage, 1)
                        assert step.n == STEPS

            def expert_block(n, s, stage):
                for j in range(ALL):
                    a, m = j % 2, ALL * n + j
                    dve.wait_ge(silued, m + 2)
                    dve.wait_ge(up, m + 1)
                    nc.vector.tensor_tensor(gu[a][:], sg[a][:], u_ps[a], ALU.mult).then_inc(multiplied, 1)
                    if j < UNITS:
                        dve.wait_ge(multiplied, m + 2)
                        dve.wait_ge(spreaded, UNITS * n + j + 1)
                        nc.vector.tensor_tensor(hid[a][:], gu[a][:], c_ps[a], ALU.mult).then_inc(hidden, 1)
                    stage(j)
                dve.wait_ge(y_done, n + 1)
                dve.wait_ge(y_stored, 16 * n)
                nc.vector.tensor_tensor(y[:], y_ps, x1[s][:], ALU.add).then_inc(y_ready, 1)

            dve.sem_inc(multiplied, 1)
            dve.sem_inc(hidden, 1)
            blocks(dve, prepare, expert_block)


INPUTS = {
    "x": (B, SQ, D), "ctxT": (B, D, SK), "wqT": (D, D), "wkT": (D, D), "wvT": (D, D), "woT": (D, D),
    "bq": (D,), "bk": (D,), "bv": (D,), "bo": (D,), "gate_wT": (D, NE), "gate_bias": (NE,),
    "w_gateT": (D, NE * NI), "w_upT": (D, NE * NI), "w_downT": (P, UNITS * D),
    "sh_gateT": (D, P), "sh_upT": (D, P), "sh_downT": (P, D),
    "ident": (P, P), "pick": (P, 2 * (DH + 1)), "spread": (3 * NE, UNITS, P),
}


def build(nc, io, out):
    ke = nc.dram_tensor("k_parts", (B, P, NCOPY, SK), BF16).ap()
    qe = nc.dram_tensor("q_parts", (B, P, NCOPY, SQ), BF16).ap()
    ve = nc.dram_tensor("v_pairs", (B, PAIRS, P, NC * VW), F32).ap()
    project(nc, io, ke, qe, ve)
    with nc.sbuf_tensor("att", [P, NPAIR + 1, QB, 2 * DH], F32) as att:
        attend(nc, io, ke, qe, ve, att)
        mix(nc, io, att, out)


def constants():
    pick = np.zeros((P, 2 * (DH + 1)), np.float32)
    for tile in range(P // VW):
        for c in range(2 * (DH + 1)):
            pick[VW * tile + c, c] = 1
    spread = np.zeros((3 * NE, UNITS, P), np.float32)
    for r in range(3 * NE):
        for m in range(P):
            if (r % NE) % EPJ == m // NI:
                spread[r, (r % NE) // EPJ, m] = 1
    return {"ident": np.eye(P, dtype=np.float32), "pick": pick, "spread": spread}


def kernel(x, ctx_1024, L0_xattn_wq, L0_xattn_bq, L0_xattn_wk, L0_xattn_bk, L0_xattn_wv, L0_xattn_bv,
           L0_xattn_wo, L0_xattn_bo, L0_ffn_gate_w, L0_ffn_gate_bias, L0_ffn_w_gate, L0_ffn_w_up,
           L0_ffn_w_down, L0_ffn_sh_gate, L0_ffn_sh_up, L0_ffn_sh_down):
    import concourse.bacc as bacc
    from concourse.bass_utils import run_bass_kernel_spmd

    host = lambda a: np.asarray(a)
    given = {
        "x": host(x), "ctxT": host(ctx_1024).transpose(0, 2, 1),
        "wqT": host(L0_xattn_wq).T, "wkT": host(L0_xattn_wk).T, "wvT": host(L0_xattn_wv).T, "woT": host(L0_xattn_wo).T,
        "bq": host(L0_xattn_bq), "bk": host(L0_xattn_bk), "bv": host(L0_xattn_bv), "bo": host(L0_xattn_bo),
        "gate_wT": host(L0_ffn_gate_w).T, "gate_bias": host(L0_ffn_gate_bias),
        "w_gateT": host(L0_ffn_w_gate).reshape(NE * NI, D).T, "w_upT": host(L0_ffn_w_up).reshape(NE * NI, D).T,
        "w_downT": host(L0_ffn_w_down).transpose(0, 2, 1).reshape(UNITS, P, D).transpose(1, 0, 2).reshape(P, UNITS * D),
        "sh_gateT": host(L0_ffn_sh_gate).T, "sh_upT": host(L0_ffn_sh_up).T, "sh_downT": host(L0_ffn_sh_down).T,
        **constants(),
    }
    nc = bacc.Bacc("TRN2", target_bir_lowering=False, num_devices=1)
    arrays, io = {}, {}
    for name, shape in INPUTS.items():
        a = np.ascontiguousarray(given[name])
        assert a.shape == shape, (name, a.shape)
        arrays[f"in_{name}"] = a
        io[name] = nc.dram_tensor(f"in_{name}", shape, mybir.dt.from_np(a.dtype), kind="ExternalInput").ap()
    out = nc.dram_tensor("out", (B, SQ, D), F32, kind="ExternalOutput").ap()
    build(nc, io, out)
    r = run_bass_kernel_spmd(nc, [arrays], core_ids=[0])
    return r.results[0]["out"]
```

```python
from contextlib import ExitStack

import numpy as np

import concourse.bass as bass
from concourse import mybir

F32 = mybir.dt.float32
BF16 = mybir.dt.bfloat16
ALU = mybir.AluOpType
ACT = mybir.ActivationFunctionType
AX = mybir.AxisListType

P = 128
B, SQ, D = 16, 256, 128
SK = 1601
NH, DH = 16, 8
QB = SQ // P
NC = (SK + P - 1) // P
LAST = SK - (NC - 1) * P
PAIRS = NH // 2
NPAIR = B * PAIRS
COPIES_K = (0, 0, 0, 1, 1, 2)
COPIES_Q = (0, 1, 2, 0, 1, 0)
NCOPY = len(COPIES_K)
ROWS = NCOPY * DH
VW = 32
NE, NI, TOPK, TOPG, NG = 32, 64, 8, 4, 8
EPJ = P // NI
UNITS = NE // EPJ
TB = 512
TT = TB // P
NBLK = B * SQ // TB
EPS = 1e-5
SCALE = 2.5
QSCALE = float(1.0 / np.sqrt(np.float32(DH)))
BANK = 512
REPLACED = -3.3e38
UNMATCHED = -3.0e38
SLOTS = 4
KEYS_OF = ((0, 401), (401, 400), (801, 400), (1201, 400))
QUARTERS = len(KEYS_OF)
ALL = UNITS + 1
PIECES = NPAIR // SLOTS - 1
PIECE = -(-3 * ALL * P // PIECES)
F32R = mybir.dt.float32r


class Steps:

    def __init__(self, eng, sem, base=0):
        self.eng, self.sem, self.base, self.n = eng, sem, base, 0

    def mark(self, ins):
        ins.then_inc(self.sem, 1)
        self.n += 1

    def wait(self):
        self.eng.wait_ge(self.sem, self.base + self.n)

    def wait_apart(self, passed):
        self.wait()
        self.eng.sem_inc(passed, 1)


def project(nc, io, ke, qe, ve, kx, qx, qm):
    with ExitStack() as ctx:
        sb = lambda name, shape, dt=F32: ctx.enter_context(nc.sbuf_tensor(name, shape, dt))
        sem = lambda name: ctx.enter_context(nc.semaphore(name))
        two = lambda name: [sem(f"{name}{s}") for s in range(2)]

        wq, wk, wv = sb("wq", [P, D]), sb("wk", [P, D]), sb("wv", [P, D])
        bqk = sb("bqk", [P, 3])
        bv = sb("bv", [P, D])
        ident = sb("ident1", [P, P])
        eps = sb("eps1", [P, 1])
        ctxt = sb("ctxt", [P, 2, SK])
        xin = sb("xin", [P, 2, QB, D])
        kr = sb("kr", [P, 2, SK])
        kp = sb("kp", [P, 2, 3, SK], BF16)
        qf, qr = sb("qf", [P, 2, SQ]), sb("qr", [P, 2, SQ])
        qp = sb("qp", [P, 2, 3, SQ], BF16)
        vs = sb("vs", [P, 2, PAIRS, NC, VW])
        st, mv = sb("st", [P, 2, QB, 6]), sb("mv", [P, 2, QB, 2])
        rs, rr = sb("rs", [P, 2, QB]), sb("rr", [P, 2, QB])
        xn, xt = sb("xn", [P, 2, QB, D]), sb("xt", [P, 2, SQ])
        ps = ctx.enter_context(nc.psum_tensor("ps1", [P, 8 * BANK], F32))
        k_ps = ps[:, 0:SK]
        v_ps = [ps[:, (4 + n) * BANK:(5 + n) * BANK].rearrange("p (c n) -> p c n", c=4) for n in range(2)]
        q_ps = ps[:, 6 * BANK:6 * BANK + SQ]
        t_ps = ps[:, 7 * BANK:7 * BANK + SQ]

        const_in, const_ready = sem("const_in"), sem("const_ready")
        ctx_in, x_in = two("ctx_in"), two("x_in")
        stored = two("stored")
        k_done, k_high, k_rest = sem("k_done"), sem("k_high"), sem("k_rest")
        k_middle, k_split, q_split = sem("k_middle"), sem("k_split"), sem("q_split")
        v_done, v_ready = sem("v_done"), sem("v_ready")
        var_ready, std_ready = sem("var_ready"), sem("std_ready")
        x_normed, x_turned, xt_ready = sem("x_normed"), sem("x_turned"), sem("xt_ready")
        q_done, q_whole, q_high = sem("q_done"), sem("q_whole"), sem("q_high")
        q_rest, q_middle = sem("q_rest"), sem("q_middle")
        dve_step, passed = sem("dve_step1"), sem("passed1")
        block = ctx.enter_context(nc.Block())
        GROUPS = [range(g, min(g + 4, NC)) for g in range(0, NC, 4)]
        NG4 = len(GROUPS)
        CONSTS = 16 * 7
        STORES = 16 * (2 * NCOPY + 1)

        @block.gpsimd
        def _(pool):
            for s in range(2):
                pool.sem_inc(stored[s], 16)
            for s in range(2):
                nc.gpsimd.memset(vs[:, s], 0.0).then_inc(const_ready, 1)
            nc.gpsimd.memset(eps[:], EPS).then_inc(const_ready, 1)
            pool.wait_ge(const_ready, 3)
            for s in range(2):
                for h in range(2):
                    nc.gpsimd.memset(vs[:, s, :, :, 9 * h + 8:9 * h + 9], 1.0).then_inc(const_ready, 1)
            with pool.Fori(0, B // 2) as i:
                for s in range(2):
                    n = 2 * i + s
                    pool.wait_ge(k_middle, n + 1)
                    nc.gpsimd.tensor_tensor(kp[:, s, 2], kr[:, s], kp[:, s, 1], ALU.subtract).then_inc(k_split, 1)
        @block.sync
        def _(sp):
            xs = io["x"].rearrange("b (t p) d -> b p t d", p=P)

            def load_x(n, s):
                sp.dma_start(xin[:, s], xs[bass.ds(n, 1)].rearrange("a p t d -> p (a t) d")).then_inc(x_in[s], 16)

            def load_ctx(n, s):
                sp.dma_start(ctxt[:, s], io["ctxT"][bass.ds(n, 1)].rearrange("a c k -> (a c) k")).then_inc(ctx_in[s], 16)

            load_x(0, 0)
            sp.dma_start(wk[:], io["wkT"]).then_inc(const_in, 16)
            load_ctx(0, 0)
            for t, name in ((wv, "wvT"), (ident, "ident"), (wq, "wqT")):
                sp.dma_start(t[:], io[name]).then_inc(const_in, 16)
            sp.dma_start(bqk[:, 0:1], io["bq"].rearrange("(d a) -> d a", a=1)).then_inc(const_in, 16)
            sp.dma_start(bqk[:, 1:2], io["bk"].rearrange("(d a) -> d a", a=1)).then_inc(const_in, 16)
            sp.dma_start(bv[:], io["bv"].partition_broadcast(P)).then_inc(const_in, 16)
            load_x(1, 1)

            def batch(i, s, last=False):
                b = 2 * i + s
                if not last:
                    sp.wait_ge(v_done, NG4 * b + 1)
                    load_ctx(b + 1, 1 - s)
                if not last and not (type(b) is int and b + 2 >= B):
                    sp.wait_ge(x_normed, b + 1)
                    load_x(b + 2, s)
                sp.wait_ge(v_ready, NG4 * (b + 1) + 2)
                sp.dma_start(ve[bass.ds(b, 1)].rearrange("a n p w -> p (a n) w"),
                             vs[:, s].rearrange("p n c w -> p n (c w)")).then_inc(stored[s], 16)
                sp.wait_ge(q_split, b + 1)
                for c, part in enumerate(COPIES_Q):
                    sp.dma_start(qe[bass.ds(b, 1), :, c].rearrange("a r q -> (a r) q"), qp[:, s, part]).then_inc(stored[s], 16)
                sp.wait_ge(k_split, b + 1)
                for c, part in enumerate(COPIES_K):
                    sp.dma_start(ke[bass.ds(b, 1), :, c].rearrange("a r k -> (a r) k"), kp[:, s, part]).then_inc(stored[s], 16)

            with sp.Fori(0, B // 2 - 1) as i:
                for s in range(2):
                    batch(i, s)
            for s in range(2):
                batch(B // 2 - 1, s, last=s == 1)
            for s in range(2):
                sp.wait_ge(stored[s], STORES * B // 2 + 16)

        @block.tensor
        def _(pe):
            pe.wait_ge(const_in, CONSTS)
            pe.sem_inc(v_done, 1)
            with pe.Fori(0, B // 2) as i:
                for s in range(2):
                    n = 2 * i + s
                    pe.wait_ge(ctx_in[s], 16 * (i + 1))
                    pe.wait_ge(k_rest, n + 1)
                    for a in range(0, SK, BANK):
                        w = min(BANK, SK - a)
                        last = nc.tensor.matmul(k_ps[:, a:a + w], wk[:], ctxt[:, s, a:a + w], start=True, stop=True)
                    last.then_inc(k_done, 1)
                    for g, chunks in enumerate(GROUPS):
                        pe.wait_ge(v_ready, NG4 * n + g + 1)
                        for c in chunks:
                            w = min(P, SK - c * P)
                            last = nc.tensor.matmul(v_ps[g % 2][0:w, c % 4], ctxt[:, s, c * P:c * P + w], wv[:], start=True, stop=True)
                        last.then_inc(v_done, 1)
                        if g == 0:
                            pe.wait_ge(x_normed, n + 1)
                            for t in range(QB):
                                last = nc.tensor.transpose(t_ps[:, t * P:(t + 1) * P], xn[:, s, t], ident[:])
                            last.then_inc(x_turned, 1)
                        if g == 2:
                            pe.wait_ge(xt_ready, n + 1)
                            pe.wait_ge(q_whole, n + 1)
                            nc.tensor.matmul(q_ps, wq[:], xt[:, s], start=True, stop=True).then_inc(q_done, 1)

        @block.scalar
        def _(act):
            act.wait_ge(const_in, CONSTS)
            act.wait_ge(const_ready, 7)
            act.sem_inc(q_whole, 1)
            nc.scalar.mul(bqk[:, 2:3], bqk[:, 0:1], QSCALE).then_inc(const_ready, 1)
            act.wait_ge(const_ready, 8)

            def deviation(n, s):
                act.wait_ge(var_ready, n + 1)
                nc.scalar.activation(rs[:, s], mv[:, s, :, 1], ACT.Sqrt, bias=eps[:]).then_inc(std_ready, 1)

            def batch(i, s, last=False):
                n = 2 * i + s
                act.wait_ge(k_done, n + 1)
                act.wait_ge(stored[s], STORES * i + 16)
                nc.scalar.activation(kp[:, s, 0], k_ps, ACT.Identity, bias=bqk[:, 1:2]).then_inc(k_high, 1)
                act.wait_ge(x_turned, n + 1)
                nc.scalar.copy(xt[:, s], t_ps).then_inc(xt_ready, 1)
                act.wait_ge(k_rest, n + 2)
                nc.scalar.copy(kp[:, s, 1], kr[:, s]).then_inc(k_middle, 1)
                if not last:
                    deviation(n + 1, 1 - s)
                act.wait_ge(q_done, n + 1)
                nc.scalar.activation(qf[:, s], q_ps, ACT.Identity, bias=bqk[:, 2:3], scale=QSCALE).then_inc(q_whole, 1)
                act.wait_ge(q_whole, n + 2)
                nc.scalar.copy(qp[:, s, 0], qf[:, s]).then_inc(q_high, 1)
                act.wait_ge(q_rest, n + 1)
                nc.scalar.copy(qp[:, s, 1], qr[:, s]).then_inc(q_middle, 1)

            deviation(0, 0)
            with act.Fori(0, B // 2 - 1) as i:
                for s in range(2):
                    batch(i, s)
            for s in range(2):
                batch(B // 2 - 1, s, last=s == 1)

        @block.vector
        def _(dve):
            dve.sem_inc(k_rest, 1)
            dve.sem_inc(v_ready, 2)
            PER = QB + 1
            step = Steps(dve, dve_step)

            def norm_a(n, s, uses):
                step.base, step.n = PER * n, 0
                dve.wait_ge(x_in[s], 16 * (uses + 1))
                for t in range(QB):
                    step.mark(nc.vector.bn_stats(st[:, s, t], xin[:, s, t]))
                step.wait_apart(passed)
                for t in range(QB):
                    last = nc.vector.bn_aggr(mv[:, s, t], st[:, s, t])
                last.then_inc(var_ready, 1)

            def norm_b(n, s):
                dve.wait_ge(std_ready, n + 1)
                step.mark(nc.vector.reciprocal(rr[:, s], rs[:, s]))
                step.wait()
                for t in range(QB):
                    last = nc.vector.tensor_scalar(xn[:, s, t], xin[:, s, t], mv[:, s, t, 0:1], rr[:, s, t:t + 1], ALU.subtract, ALU.mult)
                last.then_inc(x_normed, 1)

            def values(n, s, g):
                dve.wait_ge(v_done, NG4 * n + g + 2)
                chunks = GROUPS[g]
                w = P if g < NG4 - 1 else LAST
                for h in range(2):
                    out = vs[0:w, s, :, chunks[0]:chunks[-1] + 1, 9 * h:9 * h + DH].rearrange("p n c d -> p c n d")
                    src = v_ps[g % 2][0:w, 0:len(chunks)].rearrange("p c (n h d) -> p c n h d", h=2, d=DH)[:, :, :, h]
                    bias = bv[0:w].rearrange("p (n h d) -> p n h d", h=2, d=DH)[:, :, h].unsqueeze(1).broadcast_to([w, len(chunks), PAIRS, DH])
                    ins = nc.vector.tensor_tensor(out, src, bias, ALU.add)
                ins.then_inc(v_ready, 1)

            def batch(i, s, last=False):
                n = 2 * i + s
                dve.wait_ge(stored[s], STORES * i + 16)
                values(n, s, 0)
                values(n, s, 1)
                dve.wait_ge(k_high, n + 1)
                nc.vector.scalar_tensor_tensor(kr[:, s], k_ps, bqk[:, 1:2], kp[:, s, 0], ALU.add, ALU.subtract).then_inc(k_rest, 1)
                if not last:
                    norm_a(n + 1, 1 - s, i + s)
                values(n, s, 2)
                values(n, s, 3)
                dve.wait_ge(q_high, n + 1)
                nc.vector.tensor_tensor(qr[:, s], qf[:, s], qp[:, s, 0], ALU.subtract).then_inc(q_rest, 1)
                if not last:
                    norm_b(n + 1, 1 - s)
                dve.wait_ge(q_middle, n + 1)
                nc.vector.tensor_tensor(qp[:, s, 2], qr[:, s], qp[:, s, 1], ALU.subtract).then_inc(q_split, 1)

            norm_a(0, 0, 0)
            norm_b(0, 0)
            for s in range(SLOTS):
                nc.vector.memset(kx[s][:], 1.0)
                nc.vector.memset(qx[s][:], 0.0)
                nc.vector.memset(qm[s][:], 0.0)
            dve.wait_ge(const_in, CONSTS)
            dve.wait_ge(const_ready, 8)
            with dve.Fori(0, B // 2 - 1) as i:
                for s in range(2):
                    batch(i, s)
            for s in range(2):
                batch(B // 2 - 1, s, last=s == 1)


def attend(nc, io, ke, qe, ve, kx, qx, qm, att, wh, wl):
    with ExitStack() as ctx:
        sb = lambda name, shape, dt=F32: ctx.enter_context(nc.sbuf_tensor(name, shape, dt))
        sem = lambda name: ctx.enter_context(nc.semaphore(name))
        slots = lambda name: [sem(f"{name}{s}") for s in range(SLOTS)]

        ident = sb("ident2", [P, P])
        identb = sb("identb2", [P, P], BF16)
        pick = sb("pick", [P, 2 * (DH + 1)])
        vx = [sb(f"vx{s}", [P, NC * VW]) for s in range(SLOTS)]
        prob = [sb(f"prob{s}", [P, NC, 2 * SQ]) for s in range(2)]
        part_max = sb("part_max", [P, 2, 4, QUARTERS])
        neg, neg_rest = sb("neg", [P, 2, 4]), sb("neg_rest", [P, 2, 4])
        neg_parts = sb("neg_parts", [P, 2, 4, 3], BF16)
        neg_rows = [sb(f"neg_rows{s}", [3, 4 * P], BF16) for s in range(2)]
        ev = [sb(f"ev{s}", [P, 2 * SQ]) for s in range(2)]
        rsum = sb("rsum", [P, 2, 4])
        w_all = sb("w_all", [P, PIECES * PIECE])
        ps = ctx.enter_context(nc.psum_tensor("ps2", [P, 8 * BANK], F32))
        s_ps = [ps[:, n * BANK:(n + 1) * BANK] for n in range(3)]
        m_ps = [ps[:, n * BANK:(n + 1) * BANK] for n in range(3, 6)]
        o_ps = ps[:, 6 * BANK:7 * BANK]
        w_ps = ps[:, 7 * BANK:7 * BANK + 4 * (DH + 1)]
        t_ps = ps[:, 7 * BANK + 128:7 * BANK + 128 + 4 * P // 2].bitcast(BF16)[0:3]

        const_in, const_ready = sem("const_in2"), sem("const_ready2")
        w_in = sem("w_in")
        loaded, pair_done, neg_stored = slots("loaded"), slots("pair_done"), slots("neg_stored")
        max_scored, max_reduced = sem("max_scored"), sem("max_reduced")
        neg_ready, neg_split = sem("neg_ready"), sem("neg_split")
        neg_turned, neg_copied = sem("neg_turned"), sem("neg_copied")
        scored, exped = sem("scored"), sem("exped")
        evacuated, picked, normalised = sem("evacuated"), sem("picked"), sem("normalised")
        pool_step, dve_step, passed = sem("pool_step2"), sem("dve_step2"), sem("passed2")
        block = ctx.enter_context(nc.Block())
        MU = 4 * QUARTERS
        BODY = SLOTS * NC
        LOOPS = NPAIR // SLOTS - 1
        EVAC = 1
        WEIGHS = 2 * (NC // 4) + 1

        def of(i, t):
            return SLOTS * i + t, t % SLOTS, i + t // SLOTS

        def ring(x, body):
            return x % 3, x - 3 if x >= 3 else max(y for y in range(body) if y % 3 == x) - body

        @block.gpsimd
        def _(pool):
            nc.gpsimd.memset(w_all[:, 3 * ALL * P:], 0.0).then_inc(const_ready, 1)
            pool.wait_ge(const_in, 32)
            nc.gpsimd.tensor_copy(identb[:], ident[:]).then_inc(const_ready, 1)

            def split(i, t, step):
                n, _, _ = of(i, t)
                a = t % 2
                pool.wait_ge(neg_ready, n + 1)
                pool.sem_inc(passed, 1)
                step.mark(nc.gpsimd.tensor_copy(neg_parts[:, a, :, 0], neg[:, a]))
                step.wait()
                step.mark(nc.gpsimd.tensor_tensor(neg_rest[:, a], neg[:, a], neg_parts[:, a, :, 0], ALU.subtract))
                step.wait_apart(passed)
                step.mark(nc.gpsimd.tensor_copy(neg_parts[:, a, :, 1], neg_rest[:, a]))
                step.wait()
                nc.gpsimd.tensor_tensor(neg_parts[:, a, :, 2], neg_rest[:, a], neg_parts[:, a, :, 1], ALU.subtract).then_inc(neg_split, 1)

            first = Steps(pool, pool_step)
            split(0, 0, first)
            split(0, 1, first)
            PER = 3 * SLOTS + 1
            pool.wait_ge(w_in, 16 * 6)
            pool.wait_ge(const_ready, 3)
            with pool.Fori(0, LOOPS) as i:
                step = Steps(pool, pool_step, 6 + PER * i)
                for t in range(SLOTS):
                    split(i, t + 2, step)
                    if t == 0:
                        at = bass.ds(i * PIECE, PIECE)
                        step.mark(nc.gpsimd.tensor_copy(wh[:, at], w_all[:, at]))
                    if t == 1:
                        step.wait()
                        nc.gpsimd.tensor_tensor(wl[:, at], w_all[:, at], wh[:, at].bitcast(F32), ALU.subtract)
            i = LOOPS
            step = Steps(pool, pool_step, 6 + PER * i)
            for t in range(SLOTS - 2):
                split(i, t + 2, step)

        @block.sync
        def _(sp):
            sp.dma_start(ident[:], io["ident"]).then_inc(const_in, 16)
            sp.dma_start(pick[:], io["pick"]).then_inc(const_in, 16)
            kep = ke.rearrange("b (n h r) c k -> (b n) h (r c) k", h=2, r=DH)
            qep = qe.rearrange("b (n h r) c q -> (b n) h (r c) q", h=2, r=DH)
            vep = ve.rearrange("b n p w -> (b n) p w")

            def load(i, t):
                n, s, uses = of(i, t)
                at = bass.ds(n, 1)
                sp.wait_ge(pair_done[s], uses + 1)
                for h in range(2):
                    rows, cols = slice(64 * h, 64 * h + ROWS), slice(SQ * h, SQ * h + SQ)
                    sp.dma_start(qm[s][rows, cols], qep[at, h].rearrange("a r q -> (a r) q")).then_inc(loaded[s], 16)
                    sp.dma_start(kx[s][rows, :], kep[at, h].rearrange("a r k -> (a r) k")).then_inc(loaded[s], 16)
                    sp.dma_start(qx[s][rows, cols], qep[at, h].rearrange("a r q -> (a r) q")).then_inc(loaded[s], 16)
                sp.dma_start(vx[s][:], vep[at].rearrange("a p w -> (a p) w")).then_inc(loaded[s], 16)

            def store_neg(i, t):
                n, s, uses = of(i, t)
                sp.wait_ge(neg_copied, n + 1)
                for h in range(2):
                    sp.dma_start(qx[s][64 * h + ROWS:64 * h + ROWS + 3, SQ * h:SQ * h + SQ],
                                 neg_rows[t % 2][:, SQ * h:SQ * h + SQ]).then_inc(neg_stored[s], 16)

            for t in range(3):
                load(0, t)
            for k, (name, shared) in enumerate((("w_gateT", "sh_gateT"), ("w_upT", "sh_upT"), ("w_downT", "sh_downT"))):
                sp.dma_start(w_all[:, k * ALL * P:(k * ALL + UNITS) * P], io[name]).then_inc(w_in, 16)
                sp.dma_start(w_all[:, (k * ALL + UNITS) * P:(k + 1) * ALL * P], io[shared]).then_inc(w_in, 16)
            store_neg(0, 0)
            with sp.Fori(0, LOOPS) as i:
                for t in range(SLOTS):
                    load(i, t + 3)
                    store_neg(i, t + 1)
            i = LOOPS
            load(i, 3)
            store_neg(i, 1)
            for t in range(1, SLOTS - 1):
                store_neg(i, t + 1)

        @block.tensor
        def _(pe):
            for s in range(SLOTS):
                pe.sem_inc(pair_done[s], 1)
            pe.wait_ge(const_in, 32)
            pe.wait_ge(const_ready, 3)

            def max_unit(i, t, u, prologue=False):
                n, s, uses = of(i, t)
                x = MU * (t if prologue else t - 2) + u
                bank, before = ring(x + (MU * (SLOTS - 2) if prologue else 0), MU * SLOTS)
                if u == 0:
                    pe.wait_ge(loaded[s], 16 * 7 * (uses + 1))
                if not prologue:
                    pe.wait_ge(max_reduced, 2 * MU + MU * SLOTS * i + before + 1)
                elif x >= 3:
                    pe.wait_ge(max_reduced, x - 2)
                a, w = KEYS_OF[u % QUARTERS]
                q = u // QUARTERS
                nc.tensor.matmul(m_ps[bank][:, 0:w], qm[s][:, q * P:(q + 1) * P], kx[s][:, a:a + w],
                                 start=True, stop=True).then_inc(max_scored, 1)

            def turn_neg(i, t):
                n, _, _ = of(i, t)
                pe.wait_ge(neg_split, n + 1)
                for u in range(4):
                    last = nc.tensor.transpose(t_ps[:, u * P:(u + 1) * P], neg_parts[:, t % 2, u], identb[:])
                last.then_inc(neg_turned, 1)

            def score(i, t, c):
                n, s, uses = of(i, t)
                bank, before = ring(NC * t + c, BODY)
                if c == 0:
                    pe.wait_ge(neg_stored[s], 16 * 2 * (uses + 1))
                pe.wait_ge(exped, BODY * i + before + 1 + 3)
                w = P if c < NC - 1 else LAST
                nc.tensor.matmul(s_ps[bank][0:w, :], kx[s][:, c * P:c * P + w], qx[s][:, :], start=True, stop=True).then_inc(scored, 1)

            def weigh(i, t, k):
                n, s, uses = of(i, t)
                g, h = k // 2, k % 2
                if k == 0:
                    pe.wait_ge(evacuated, n + 1)
                for j in range(4):
                    c = min(4 * g + j, NC - 1)
                    if h == 0 and (c < NC - 1 or j == 0):
                        pe.wait_ge(exped, BODY * i + NC * t + c + 1 + 3)
                    w, cols = (P, slice(SQ * h, SQ * h + SQ)) if c < NC - 1 else (LAST, slice(j * P, (j + 1) * P))
                    last = nc.tensor.matmul(o_ps[32 * j:32 * j + VW, cols], vx[s][0:w, c * VW:(c + 1) * VW], prob[t % 2][0:w, c, cols],
                                            start=k == 0, stop=c == NC - 1, skip_group_check=True)
                if k == WEIGHS - 1:
                    last.then_inc(pair_done[s], 1)

            def pick_out(i, t):
                n, _, _ = of(i, t)
                pe.wait_ge(evacuated, n + 1)
                pe.wait_ge(normalised, n + 1)
                for u in range(4):
                    h = u // 2
                    last = nc.tensor.matmul(w_ps[:, u * (DH + 1):(u + 1) * (DH + 1)], ev[(t - 1) % 2][:, u * P:(u + 1) * P],
                                            pick[:, h * (DH + 1):(h + 1) * (DH + 1)], start=True, stop=True)
                last.then_inc(picked, 1)

            ORDER = "SMSMSMMSMOSMSWMSMTMSWMSMSWMSMMSWMSMWWW"

            def pair(i, t, turn=True, ahead=True):
                n, _, _ = of(i, t)
                c = u = g = 0
                for what in ORDER:
                    if what == "S":
                        score(i, t, c)
                        c += 1
                    elif what == "M":
                        if ahead:
                            max_unit(i, t + 2, u)
                        u += 1
                    elif what == "W":
                        weigh(i, t, g)
                        g += 1
                    elif what == "O":
                        pe.wait_ge(neg_copied, n + 1)
                        pick_out(i, t)
                    elif turn:
                        pe.wait_ge(normalised, n + 2)
                        turn_neg(i, t + 1)
                assert (c, u, g) == (NC, MU, WEIGHS)

            for t in range(2):
                for u in range(MU):
                    max_unit(0, t, u, prologue=True)
            turn_neg(0, 0)
            with pe.Fori(0, LOOPS) as i:
                for t in range(SLOTS):
                    pair(i, t)
            i = LOOPS
            for t in range(SLOTS):
                pair(i, t, turn=t + 1 < SLOTS, ahead=t + 2 < SLOTS)
            pick_out(i, SLOTS)

        @block.scalar
        def _(act):
            act.wait_ge(const_ready, 3)
            act.sem_inc(exped, 3)

            def copy_neg(i, t):
                n, _, _ = of(i, t)
                act.wait_ge(neg_turned, n + 1)
                nc.scalar.copy(neg_rows[t % 2][:], t_ps).then_inc(neg_copied, 1)

            def evacuate(i, t):
                _, s, uses = of(i, t - 1)
                act.wait_ge(pair_done[s], uses + 2)
                nc.scalar.copy(ev[(t - 1) % 2][:], o_ps).then_inc(evacuated, 1)

            def pair(i, t, turn=True):
                n, s, uses = of(i, t)
                for c in range(NC):
                    if c == EVAC:
                        evacuate(i, t)
                    act.wait_ge(scored, NC * n + c + 1)
                    w = P if c < NC - 1 else LAST
                    bank, _ = ring(NC * t + c, BODY)
                    nc.scalar.activation(prob[t % 2][0:w, c], s_ps[bank][0:w, :], ACT.Exp).then_inc(exped, 1)
                    if c == 6 and turn:
                        copy_neg(i, t + 1)

            copy_neg(0, 0)
            with act.Fori(0, LOOPS) as i:
                for t in range(SLOTS):
                    pair(i, t)
            i = LOOPS
            for t in range(SLOTS):
                pair(i, t, turn=t + 1 < SLOTS)
            evacuate(i, SLOTS)

        @block.vector
        def _(dve):
            dve.sem_inc(normalised, 1)
            nc.vector.memset(o_ps, 1.0).then_inc(const_ready, 1)

            def reduce_unit(i, t, u, prologue=False):
                n, _, _ = of(i, t)
                x = MU * (t + SLOTS - 2 if prologue else t - 2) + u
                bank, _ = ring(x, MU * SLOTS)
                q, k = u // QUARTERS, u % QUARTERS
                dve.wait_ge(max_scored, MU * n + u + 1)
                nc.vector.tensor_reduce(part_max[:, t % 2, q, k:k + 1], m_ps[bank][:, 0:KEYS_OF[k][1]],
                                        AX.X, ALU.max).then_inc(max_reduced, 1)

            def negate(i, t):
                n, _, _ = of(i, t)
                dve.wait_ge(max_reduced, MU * (n + 1))
                nc.vector.tensor_reduce(neg[:, t % 2], part_max[:, t % 2], AX.X, ALU.max, negate=True).then_inc(neg_ready, 1)

            def normalise(i, t, step):
                n, _, _ = of(i, t)
                dve.wait_ge(picked, n + 1)
                out = w_ps.rearrange("p (u r) -> p u r", u=4)
                step.mark(nc.vector.reciprocal(rsum[:, t % 2].unsqueeze(2), out[:, :, DH:DH + 1]))
                step.wait()
                to = att[:, bass.ds(n, 1)].rearrange("p a b (h d) -> p (a h) b d", h=2)
                nc.vector.tensor_tensor(to, out[:, :, 0:DH].rearrange("p (h b) d -> p h b d", h=2),
                                        rsum[:, t % 2].rearrange("p (h b) -> p h b", h=2).unsqueeze(3).broadcast_to([P, 2, QB, DH]),
                                        ALU.mult).then_inc(normalised, 1)

            def pair(i, t, step, ahead=True):
                for u in range(MU):
                    if ahead:
                        reduce_unit(i, t + 2, u)
                    if u == 4:
                        normalise(i, t, step)
                if ahead:
                    negate(i, t + 2)

            for t in range(2):
                for u in range(MU):
                    reduce_unit(0, t, u, prologue=True)
                negate(0, t)
            with dve.Fori(0, LOOPS) as i:
                step = Steps(dve, dve_step, SLOTS * i)
                for t in range(SLOTS):
                    pair(i, t, step)
            i = LOOPS
            step = Steps(dve, dve_step, SLOTS * i)
            for t in range(SLOTS):
                pair(i, t, step, ahead=t + 2 < SLOTS)
            normalise(i, SLOTS, step)


def mix(nc, io, att, out):
    with ExitStack() as ctx:
        sb = lambda name, shape, dt=F32: ctx.enter_context(nc.sbuf_tensor(name, shape, dt))
        sem = lambda name: ctx.enter_context(nc.semaphore(name))

        ident = sb("ident3", [P, P])
        identb = sb("identb3", [P, P], BF16)
        wo, gw = sb("wo", [P, D]), sb("gw", [P, NE])
        bo, gb = sb("bo", [P, D]), sb("gb", [P, NE])
        eps = sb("eps3", [P, 1])
        wg, wu = sb("wg", [P, UNITS + 1, P]), sb("wu", [P, UNITS + 1, P])
        wd = sb("wd", [P, UNITS + 1, D])
        spread_f = sb("spread_f", [3 * NE, UNITS, P])
        spread = sb("spread", [3 * NE, UNITS, P], BF16)
        x1 = [sb(f"x1{s}", [P, TT, D]) for s in range(2)]
        ht = [sb(f"ht{s}", [P, TB]) for s in range(2)]
        ct = [sb(f"ct{s}", [3 * NE, TB], BF16) for s in range(2)]
        xin = sb("xin3", [P, TT, D])
        ob, ot = sb("ob", [P, TT, D]), sb("ot", [P, TB])
        st, mv, rs = sb("st3", [P, TT, 6]), sb("mv3", [P, TT, 2]), sb("rs3", [P, TT])
        hn = sb("hn", [P, TT, D])
        score = sb("score", [P, TT, NE])
        biased, masked, left = sb("biased", [P, TT, NE]), sb("masked", [P, TT, NE]), sb("left", [P, TT, NE])
        hi, lo = sb("hi", [P, TT * NG, 2]), sb("lo", [P, TT * NG, 2])
        top, second = sb("top", [P, TT * NG]), sb("second", [P, TT * NG])
        gscore, gleft = sb("gscore", [P, TT, NG]), sb("gleft", [P, TT, NG])
        best = sb("best", [P, TT, 8])
        total = sb("total", [P, TT])
        cw, cr = sb("cw", [P, TT, NE]), sb("cr", [P, TT, NE])
        cp = sb("cp", [P, TT, 3, NE], BF16)
        sg = [sb(f"sg{n}", [P, TB]) for n in range(2)]
        gu = [sb(f"gu{n}", [P, TB]) for n in range(2)]
        hid = [sb(f"hid{n}", [P, TB]) for n in range(2)]
        y = sb("y", [P, TT, D])
        ps = ctx.enter_context(nc.psum_tensor("ps3", [P, 8 * BANK], F32))
        bank = lambda n: ps[:, n * BANK:(n + 1) * BANK]
        g_ps, u_ps, c_ps = [bank(0), bank(1)], [bank(2), bank(3)], [bank(4), bank(5)]
        y_ps = bank(6).rearrange("p (t d) -> p t d", t=TT)
        z_ps = bank(7)
        z_tiles = z_ps.rearrange("p (t d) -> p t d", t=TT)
        z_bf = z_ps.bitcast(BF16)[0:3 * NE, 0:TB]

        const_in, const_ready = sem("const_in3"), sem("const_ready3")
        x_in, ob_ready = sem("x_in3"), sem("ob_ready")
        pe_stage, act_stage, dve_stage = sem("pe_stage"), sem("act_stage"), sem("dve_stage")
        gated, up, spreaded = sem("gated"), sem("up"), sem("spreaded")
        silued, multiplied, hidden = sem("silued"), sem("multiplied"), sem("hidden")
        y_done, y_ready, y_stored = sem("y_done"), sem("y_ready"), sem("y_stored")
        dve_step, passed, gathers = sem("dve_step3"), sem("passed3"), sem("gathers")
        block = ctx.enter_context(nc.Block())
        ALL = UNITS + 1
        PE_ST, ACT_ST, DVE_ST = 5, 5, 4
        CONSTS = 12
        STEPS = 44

        def blocks(eng, prepare, expert_block):
            for k in range(ALL):
                prepare(0, 0, k)
            with eng.Fori(0, NBLK // 2 - 1) as i:
                for s in range(2):
                    expert_block(2 * i + s, s, lambda k: prepare(2 * i + s + 1, 1 - s, k))
            expert_block(NBLK - 2, 0, lambda k: prepare(NBLK - 1, 1, k))
            expert_block(NBLK - 1, 1, lambda k: None)

        @block.gpsimd
        def _(pool):
            nc.gpsimd.memset(eps[:], EPS).then_inc(const_ready, 1)
            pool.wait_ge(const_in, 16 * CONSTS)
            nc.gpsimd.tensor_copy(identb[:], ident[:]).then_inc(const_ready, 1)
            nc.gpsimd.tensor_copy(spread[:], spread_f[:]).then_inc(const_ready, 1)

            def gather(n):
                for b2 in range(TT // QB):
                    src = att[:, bass.ds(1 + n * (PAIRS * TT // QB) + b2 * PAIRS, PAIRS)].rearrange("p a b c -> p b a c")
                    ins = nc.gpsimd.tensor_copy(ob[:, b2 * QB:(b2 + 1) * QB].rearrange("p b (a c) -> p b a c", a=PAIRS), src)
                ins.then_inc(ob_ready, 1)

            gather(0)
            with pool.Fori(1, NBLK) as n:
                pool.wait_ge(pe_stage, PE_ST * n - PE_ST + 1)
                pool.sem_inc(gathers, 1)
                gather(n)

        @block.sync
        def _(sp):
            xt = io["x"].rearrange("b (t p) d -> p (b t) d", p=P)
            ot_ = out.rearrange("b (t p) d -> p (b t) d", p=P)
            for t, name in ((ident, "ident"), (wo, "woT"), (gw, "gate_wT"), (spread_f, "spread")):
                sp.dma_start(t[:], io[name]).then_inc(const_in, 16)
            sp.dma_start(bo[:], io["bo"].partition_broadcast(P)).then_inc(const_in, 16)
            sp.dma_start(gb[:], io["gate_bias"].partition_broadcast(P)).then_inc(const_in, 16)
            sp.dma_start(xin[:], xt[:, 0:TT]).then_inc(x_in, 16)
            for t, name, shared in ((wg, "w_gateT", "sh_gateT"), (wu, "w_upT", "sh_upT"), (wd, "w_downT", "sh_downT")):
                sp.dma_start(t[:, 0:UNITS], io[name].rearrange("p (j n) -> p j n", n=P)).then_inc(const_in, 16)
                sp.dma_start(t[:, UNITS], io[shared]).then_inc(const_in, 16)

            def store(n):
                sp.wait_ge(y_ready, n + 2)
                sp.dma_start(ot_[:, bass.ds(TT * n, TT)], y[:]).then_inc(y_stored, 16)

            with sp.Fori(0, NBLK - 1) as n:
                sp.wait_ge(dve_stage, DVE_ST * n + 1)
                sp.dma_start(xin[:], xt[:, bass.ds(TT * n + TT, TT)]).then_inc(x_in, 16)
                store(n)
            store(NBLK - 1)
            sp.wait_ge(y_stored, 16 * NBLK + 16)

        @block.tensor
        def _(pe):
            pe.wait_ge(const_in, 16 * CONSTS)
            pe.wait_ge(const_ready, 3)

            def prepare(n, s, k):
                if k == 0:
                    pe.wait_ge(ob_ready, n + 1)
                    for t in range(TT):
                        last = nc.tensor.transpose(z_tiles[:, t], ob[:, t], ident[:])
                elif k == 2:
                    pe.wait_ge(act_stage, ACT_ST * n + 1)
                    for t in range(TT):
                        last = nc.tensor.matmul(z_tiles[:, t], ot[:, t * P:(t + 1) * P], wo[:], start=True, stop=True)
                elif k == 7:
                    pe.wait_ge(dve_stage, DVE_ST * n + 3)
                    for t in range(TT):
                        last = nc.tensor.transpose(z_tiles[:, t], hn[:, t], ident[:])
                elif k == 9:
                    pe.wait_ge(act_stage, ACT_ST * n + 3)
                    for t in range(TT):
                        last = nc.tensor.matmul(z_ps[:, t * NE:(t + 1) * NE], ht[s][:, t * P:(t + 1) * P], gw[:], start=True, stop=True)
                elif k == 14:
                    pe.wait_ge(dve_stage, DVE_ST * n + 4)
                    for t in range(TT):
                        last = nc.tensor.transpose(z_bf[:, t * P:(t + 1) * P], cp[:, t].rearrange("p c e -> p (c e)"), identb[:])
                else:
                    return
                last.then_inc(pe_stage, 1)

            def down(n, j):
                if j == 0:
                    pe.wait_ge(y_ready, n + 1)
                if j < UNITS:
                    pe.wait_ge(hidden, UNITS * n + j + 3)
                else:
                    pe.wait_ge(multiplied, ALL * n + j + 2)
                act_in = hid[j % 2] if j < UNITS else gu[j % 2]
                for t in range(TT):
                    last = nc.tensor.matmul(y_ps[:, t], act_in[:, t * P:(t + 1) * P], wd[:, j],
                                            start=j == 0 and t == 0, stop=j == ALL - 1, skip_group_check=True)
                if j == ALL - 1:
                    last.then_inc(y_done, 1)

            def expert_block(n, s, stage):
                for j in range(ALL):
                    if j == 0:
                        pe.wait_ge(act_stage, ACT_ST * (n + 1))
                    a, m = j % 2, ALL * n + j
                    free = m + (j == 0)
                    pe.wait_ge(silued, free)
                    nc.tensor.matmul(g_ps[a], wg[:, j], ht[s][:], start=True, stop=True).then_inc(gated, 1)
                    pe.wait_ge(multiplied, free)
                    nc.tensor.matmul(u_ps[a], wu[:, j], ht[s][:], start=True, stop=True).then_inc(up, 1)
                    if j < UNITS:
                        pe.wait_ge(hidden, UNITS * n + j + 1)
                        nc.tensor.matmul(c_ps[a], spread[:, j], ct[s][:], start=True, stop=True).then_inc(spreaded, 1)
                    if j:
                        down(n, j - 1)
                    stage(j)
                down(n, ALL - 1)

            blocks(pe, prepare, expert_block)

        @block.scalar
        def _(act):
            act.wait_ge(const_ready, 3)

            def prepare(n, s, k):
                if k == 1:
                    act.wait_ge(pe_stage, PE_ST * n + 1)
                    ins = nc.scalar.copy(ot[:], z_ps)
                elif k == 5:
                    act.wait_ge(dve_stage, DVE_ST * n + 2)
                    ins = nc.scalar.activation(rs[:], mv[:, :, 1], ACT.Sqrt, bias=eps[:])
                elif k == 8:
                    act.wait_ge(pe_stage, PE_ST * n + 3)
                    ins = nc.scalar.copy(ht[s][:], z_ps)
                elif k == 10:
                    act.wait_ge(pe_stage, PE_ST * n + 4)
                    ins = nc.scalar.activation(score[:].rearrange("p t e -> p (t e)"), z_ps[:, 0:TT * NE], ACT.Exp, scale=-1.0)
                elif k == 15:
                    act.wait_ge(pe_stage, PE_ST * n + 5)
                    ins = nc.scalar.copy(ct[s][:], z_bf)
                else:
                    return
                ins.then_inc(act_stage, 1)

            def expert_block(n, s, stage):
                for j in range(ALL):
                    m = ALL * n + j
                    act.wait_ge(gated, m + 1)
                    act.wait_ge(multiplied, m + (j == 0))
                    nc.scalar.activation(sg[j % 2][:], g_ps[j % 2], ACT.Silu).then_inc(silued, 1)
                    stage(j)

            act.sem_inc(silued, 1)
            blocks(act, prepare, expert_block)

        @block.vector
        def _(dve):
            dve.wait_ge(const_in, 16 * CONSTS)

            step = Steps(dve, dve_step)

            def prepare(n, s, k):
                    flat = lambda t: t[:].rearrange("p t e -> p (t e)")
                    if k == 3:
                        step.base, step.n = STEPS * n, 0
                        dve.wait_ge(x_in, 16 * (n + 1))
                        dve.wait_ge(pe_stage, PE_ST * n + 2)
                        nc.vector.tensor_tensor(x1[s][:], z_tiles, xin[:], ALU.add).then_inc(dve_stage, 1)
                        dve.wait_ge(dve_stage, DVE_ST * n + 1)
                        step.mark(nc.vector.tensor_tensor(x1[s][:], x1[s][:], bo[:].unsqueeze(1).broadcast_to([P, TT, D]), ALU.add))
                    elif k == 4:
                        step.wait()
                        for t in range(TT):
                            step.mark(nc.vector.bn_stats(st[:, t], x1[s][:, t]))
                        step.wait_apart(passed)
                        for t in range(TT):
                            last = nc.vector.bn_aggr(mv[:, t], st[:, t])
                        last.then_inc(dve_stage, 1)
                    elif k == 6:
                        dve.wait_ge(act_stage, ACT_ST * n + 2)
                        step.mark(nc.vector.reciprocal(rs[:], rs[:]))
                        step.wait()
                        for t in range(TT):
                            last = nc.vector.tensor_scalar(hn[:, t], x1[s][:, t], mv[:, t, 0:1], rs[:, t:t + 1], ALU.subtract, ALU.mult)
                        last.then_inc(dve_stage, 1)
                    elif k == 11:
                        dve.wait_ge(act_stage, ACT_ST * n + 4)
                        step.mark(nc.vector.tensor_scalar(score[:], score[:], 1.0, None, ALU.add))
                        step.wait()
                        step.mark(nc.vector.reciprocal(score[:], score[:]))
                        step.wait()
                        step.mark(nc.vector.tensor_tensor(biased[:], score[:], gb[:].unsqueeze(1).broadcast_to([P, TT, NE]), ALU.add))
                        step.wait()
                        four = flat(biased).rearrange("p (g a b) -> p g a b", a=2, b=2)
                        step.mark(nc.vector.tensor_tensor(hi[:], four[:, :, :, 0], four[:, :, :, 1], ALU.max))
                        step.mark(nc.vector.tensor_tensor(lo[:], four[:, :, :, 0], four[:, :, :, 1], ALU.min))
                        step.wait()
                        step.mark(nc.vector.tensor_tensor(top[:], hi[:, :, 0], hi[:, :, 1], ALU.max))
                        step.mark(nc.vector.tensor_tensor(second[:], hi[:, :, 0], hi[:, :, 1], ALU.min))
                        step.mark(nc.vector.tensor_tensor(lo[:, :, 0], lo[:, :, 0], lo[:, :, 1], ALU.max))
                        step.wait()
                        step.mark(nc.vector.tensor_tensor(second[:], second[:], lo[:, :, 0], ALU.max))
                        step.wait()
                        step.mark(nc.vector.tensor_tensor(flat(gscore), top[:], second[:], ALU.add))
                    elif k == 12:
                        step.wait_apart(passed)
                        for t in range(TT):
                            step.mark(nc.vector.max(best[:, t], gscore[:, t]))
                        step.wait()
                        step.mark(nc.vector.memset(best[:, :, TOPG:8], UNMATCHED))
                        step.wait_apart(passed)
                        for t in range(TT):
                            step.mark(nc.vector.match_replace(gleft[:, t], best[:, t], gscore[:, t], REPLACED))
                        step.wait()
                        step.mark(nc.vector.tensor_tensor(gleft[:], gleft[:], gscore[:], ALU.is_lt))
                        step.wait()
                        step.mark(nc.vector.tensor_tensor(flat(masked).rearrange("p (g e) -> p g e", e=NE // NG),
                                                          flat(biased).rearrange("p (g e) -> p g e", e=NE // NG),
                                                          flat(gleft).unsqueeze(2).broadcast_to([P, TT * NG, NE // NG]), ALU.mult))
                        step.wait_apart(passed)
                        for t in range(TT):
                            step.mark(nc.vector.max(best[:, t], masked[:, t]))
                    elif k == 13:
                        step.wait_apart(passed)
                        for t in range(TT):
                            step.mark(nc.vector.match_replace(left[:, t], best[:, t], masked[:, t], REPLACED))
                        step.wait()
                        step.mark(nc.vector.tensor_tensor(left[:], left[:], masked[:], ALU.is_lt))
                        step.wait()
                        step.mark(nc.vector.tensor_tensor(cw[:], score[:], left[:], ALU.mult))
                        step.wait()
                        step.mark(nc.vector.tensor_reduce(total[:], cw[:], AX.X, ALU.add))
                        step.wait()
                        step.mark(nc.vector.tensor_scalar(total[:], total[:], 1e-20, None, ALU.add))
                        step.wait()
                        step.mark(nc.vector.reciprocal(total[:], total[:]))
                        step.wait()
                        step.mark(nc.vector.scalar_tensor_tensor(cw[:], cw[:], SCALE, total[:].unsqueeze(2).broadcast_to([P, TT, NE]), ALU.mult, ALU.mult))
                        step.wait()
                        step.mark(nc.vector.tensor_copy(cp[:, :, 0], cw[:]))
                        step.wait()
                        step.mark(nc.vector.tensor_tensor(cr[:], cw[:], cp[:, :, 0], ALU.subtract))
                        step.wait()
                        step.mark(nc.vector.tensor_copy(cp[:, :, 1], cr[:]))
                        step.wait()
                        nc.vector.tensor_tensor(cp[:, :, 2], cr[:], cp[:, :, 1], ALU.subtract).then_inc(dve_stage, 1)
                        assert step.n == STEPS

            def expert_block(n, s, stage):
                for j in range(ALL):
                    a, m = j % 2, ALL * n + j
                    dve.wait_ge(silued, m + 2)
                    dve.wait_ge(up, m + 1)
                    nc.vector.tensor_tensor(gu[a][:], sg[a][:], u_ps[a], ALU.mult).then_inc(multiplied, 1)
                    if j < UNITS:
                        dve.wait_ge(multiplied, m + 2)
                        dve.wait_ge(spreaded, UNITS * n + j + 1)
                        nc.vector.tensor_tensor(hid[a][:], gu[a][:], c_ps[a], ALU.mult).then_inc(hidden, 1)
                    stage(j)
                dve.wait_ge(y_done, n + 1)
                dve.wait_ge(y_stored, 16 * n + 16)
                nc.vector.tensor_tensor(y[:], y_ps, x1[s][:], ALU.add).then_inc(y_ready, 1)

            dve.sem_inc(multiplied, 1)
            dve.sem_inc(hidden, 2)
            dve.sem_inc(y_ready, 1)
            dve.sem_inc(y_stored, 16)
            blocks(dve, prepare, expert_block)


INPUTS = {
    "x": (B, SQ, D), "ctxT": (B, D, SK), "wqT": (D, D), "wkT": (D, D), "wvT": (D, D), "woT": (D, D),
    "bq": (D,), "bk": (D,), "bv": (D,), "bo": (D,), "gate_wT": (D, NE), "gate_bias": (NE,),
    "w_gateT": (D, NE * NI), "w_upT": (D, NE * NI), "w_downT": (P, UNITS * D),
    "sh_gateT": (D, P), "sh_upT": (D, P), "sh_downT": (P, D),
    "ident": (P, P), "pick": (P, 2 * (DH + 1)), "spread": (3 * NE, UNITS, P),
}


def build(nc, io, out):
    ke = nc.dram_tensor("k_parts", (B, P, NCOPY, SK), BF16).ap()
    qe = nc.dram_tensor("q_parts", (B, P, NCOPY, SQ), BF16).ap()
    ve = nc.dram_tensor("v_pairs", (B, PAIRS, P, NC * VW), F32).ap()
    with ExitStack() as ctx:
        sb = lambda name, shape, dt=F32: ctx.enter_context(nc.sbuf_tensor(name, shape, dt))
        att = sb("att", [P, NPAIR + 1, QB, 2 * DH])
        wh, wl = sb("wh", [P, PIECES * PIECE], F32R), sb("wl", [P, PIECES * PIECE], F32R)
        with ExitStack() as operands:
            slots = lambda name, width: [operands.enter_context(nc.sbuf_tensor(f"{name}{s}", [P, width], BF16)) for s in range(SLOTS)]
            kx, qx, qm = slots("kx", SK), slots("qx", 2 * SQ), slots("qm", 2 * SQ)
            project(nc, io, ke, qe, ve, kx, qx, qm)
            attend(nc, io, ke, qe, ve, kx, qx, qm, att, wh, wl)
        mix(nc, io, att, out)


def constants():
    pick = np.zeros((P, 2 * (DH + 1)), np.float32)
    for tile in range(P // VW):
        for c in range(2 * (DH + 1)):
            pick[VW * tile + c, c] = 1
    spread = np.zeros((3 * NE, UNITS, P), np.float32)
    for r in range(3 * NE):
        for m in range(P):
            if (r % NE) % EPJ == m // NI:
                spread[r, (r % NE) // EPJ, m] = 1
    return {"ident": np.eye(P, dtype=np.float32), "pick": pick, "spread": spread}


def kernel(x, ctx_1024, L0_xattn_wq, L0_xattn_bq, L0_xattn_wk, L0_xattn_bk, L0_xattn_wv, L0_xattn_bv,
           L0_xattn_wo, L0_xattn_bo, L0_ffn_gate_w, L0_ffn_gate_bias, L0_ffn_w_gate, L0_ffn_w_up,
           L0_ffn_w_down, L0_ffn_sh_gate, L0_ffn_sh_up, L0_ffn_sh_down):
    import concourse.bacc as bacc
    from concourse.bass_utils import run_bass_kernel_spmd

    host = lambda a: np.asarray(a)
    given = {
        "x": host(x), "ctxT": host(ctx_1024).transpose(0, 2, 1),
        "wqT": host(L0_xattn_wq).T, "wkT": host(L0_xattn_wk).T, "wvT": host(L0_xattn_wv).T, "woT": host(L0_xattn_wo).T,
        "bq": host(L0_xattn_bq), "bk": host(L0_xattn_bk), "bv": host(L0_xattn_bv), "bo": host(L0_xattn_bo),
        "gate_wT": host(L0_ffn_gate_w).T, "gate_bias": host(L0_ffn_gate_bias),
        "w_gateT": host(L0_ffn_w_gate).reshape(NE * NI, D).T, "w_upT": host(L0_ffn_w_up).reshape(NE * NI, D).T,
        "w_downT": host(L0_ffn_w_down).transpose(0, 2, 1).reshape(UNITS, P, D).transpose(1, 0, 2).reshape(P, UNITS * D),
        "sh_gateT": host(L0_ffn_sh_gate).T, "sh_upT": host(L0_ffn_sh_up).T, "sh_downT": host(L0_ffn_sh_down).T,
        **constants(),
    }
    nc = bacc.Bacc("TRN2", target_bir_lowering=False, num_devices=1)
    arrays, io = {}, {}
    for name, shape in INPUTS.items():
        a = np.ascontiguousarray(given[name])
        assert a.shape == shape, (name, a.shape)
        arrays[f"in_{name}"] = a
        io[name] = nc.dram_tensor(f"in_{name}", shape, mybir.dt.from_np(a.dtype), kind="ExternalInput").ap()
    out = nc.dram_tensor("out", (B, SQ, D), F32, kind="ExternalOutput").ap()
    build(nc, io, out)
    r = run_bass_kernel_spmd(nc, [arrays], core_ids=[0])
    return r.results[0]["out"]
```

```python
from contextlib import ExitStack

import numpy as np

import concourse.bass as bass
from concourse import mybir

F32 = mybir.dt.float32
BF16 = mybir.dt.bfloat16
ALU = mybir.AluOpType
ACT = mybir.ActivationFunctionType
AX = mybir.AxisListType

P = 128
B, SQ, D = 16, 256, 128
SK = 1601
NH, DH = 16, 8
QB = SQ // P
NC = (SK + P - 1) // P
LAST = SK - (NC - 1) * P
PAIRS = NH // 2
NPAIR = B * PAIRS
PARTS = 3
COPIES_Q = (0, 0, 1, 1, 2, 0)
NCOPY = len(COPIES_Q)
ROWS = NCOPY * DH
VC = 2 * (DH + 1)
VW = 32
NE, NI, TOPK, TOPG, NG = 32, 64, 8, 4, 8
EPJ = P // NI
UNITS = NE // EPJ
TB = 512
TT = TB // P
NBLK = B * SQ // TB
EPS = 1e-5
SCALE = 2.5
QSCALE = float(1.0 / np.sqrt(np.float32(DH)))
BANK = 512
REPLACED = -3.3e38
UNMATCHED = -3.0e38
SLOTS = 4
CT = P // VW
KEYS_OF = ((0, 401), (401, 400), (801, 400), (1201, 400))
QUARTERS = len(KEYS_OF)
ALL = UNITS + 1
PIECES = B - 1
PIECE = -(-3 * ALL * P // PIECES)
F32R = mybir.dt.float32r


class Steps:

    def __init__(self, eng, sem, base=0):
        self.eng, self.sem, self.base, self.n = eng, sem, base, 0

    def mark(self, ins):
        ins.then_inc(self.sem, 1)
        self.n += 1

    def wait(self):
        self.eng.wait_ge(self.sem, self.base + self.n)

    def wait_apart(self, passed):
        self.wait()
        self.eng.sem_inc(passed, 1)


class Kept:

    def __init__(self, sb):
        self.ident, self.identb = sb("ident", [P, P]), sb("identb", [P, P], BF16)
        self.pick = sb("pick", [P, 2, 4, VW])
        self.wo, self.gw = sb("wo", [P, D]), sb("gw", [P, NE])
        self.bo, self.gb = sb("bo", [P, D]), sb("gb", [P, NE])
        self.eps = sb("eps", [P, 1])
        self.spread = sb("spread", [3 * NE, UNITS, P], BF16)
        self.xin = sb("x_block", [P, TT, D])


class Operands:

    def __init__(self, sb, sem):
        slots = lambda name, width, dt=BF16: [sb(f"{name}{s}", [P, width], dt) for s in range(SLOTS)]
        self.kx, self.qx, self.qm, self.vx = slots("kx", SK), slots("qx", 2 * SQ), slots("qm", 2 * SQ), slots("vx", NC * VC, F32)
        self.loaded = [sem(f"loaded{s}") for s in range(SLOTS)]

    def load(self, sp, ke, qe, ve, n, s):
        pairs_heads = [[2 * PARTS * DH * SK, NPAIR], [PARTS * DH * SK, 2]]
        twice = bass.AP(tensor=ke.tensor, offset=0, ap=pairs_heads + [[0, 2], [SK, 2 * DH], [1, SK]])
        ends = bass.AP(tensor=ke.tensor, offset=0, ap=pairs_heads + [[2 * DH * SK, 2], [SK, DH], [1, SK]])
        qep = qe.rearrange("b (n h) c r q -> (b n) h (c r) q", h=2)
        vep = ve.rearrange("b n p w -> (b n) p w")
        at = bass.ds(n, 1)
        for h in range(2):
            rows, cols = slice(64 * h, 64 * h + ROWS), slice(SQ * h, SQ * h + SQ)
            sp.dma_start(self.qm[s][rows, cols], qep[at, h].rearrange("a r q -> (a r) q")).then_inc(self.loaded[s], 16)
            sp.dma_start(self.kx[s][64 * h:64 * h + 4 * DH, :], twice[at, h].squeeze(0)).then_inc(self.loaded[s], 16)
            sp.dma_start(self.kx[s][64 * h + 4 * DH:64 * h + ROWS, :], ends[at, h].squeeze(0)).then_inc(self.loaded[s], 16)
            sp.dma_start(self.qx[s][rows, cols], qep[at, h].rearrange("a r q -> (a r) q")).then_inc(self.loaded[s], 16)
        sp.dma_start(self.vx[s][:], vep[at].rearrange("a p w -> (a p) w")).then_inc(self.loaded[s], 16)


def project(nc, io, ke, qe, ve, kept, operands):
    with ExitStack() as ctx:
        sb = lambda name, shape, dt=F32: ctx.enter_context(nc.sbuf_tensor(name, shape, dt))
        sem = lambda name: ctx.enter_context(nc.semaphore(name))
        two = lambda name: [sem(f"{name}{s}") for s in range(2)]

        wq, wk, wv = sb("wq", [P, D]), sb("wk", [P, D]), sb("wv", [P, D])
        bqk = sb("bqk", [P, 3])
        bv = sb("bv", [P, D])
        ident, eps = kept.ident, kept.eps
        spread_f = sb("spread_f", [3 * NE, UNITS, P])
        ctxt = sb("ctxt", [P, 2, SK])
        xin = sb("xin", [P, 2, QB, D])
        kr = sb("kr", [P, 2, SK])
        kp = sb("kp", [P, 2, 3, SK], BF16)
        qf, qr = sb("qf", [P, 2, SQ]), sb("qr", [P, 2, SQ])
        qp = sb("qp", [P, 2, 3, SQ], BF16)
        vs = sb("vs", [P, 2, PAIRS, NC, VC])
        st, mv = sb("st", [P, 2, QB, 6]), sb("mv", [P, 2, QB, 2])
        rs, rr = sb("rs", [P, 2, QB]), sb("rr", [P, 2, QB])
        xn, xt = sb("xn", [P, 2, QB, D]), sb("xt", [P, 2, SQ])
        ps = ctx.enter_context(nc.psum_tensor("ps1", [P, 8 * BANK], F32))
        k_ps = ps[:, 0:SK]
        v_ps = [ps[:, (4 + n) * BANK:(5 + n) * BANK].rearrange("p (c n) -> p c n", c=4) for n in range(2)]
        q_ps = ps[:, 6 * BANK:6 * BANK + SQ]
        t_ps = ps[:, 7 * BANK:7 * BANK + SQ]

        const_in, const_ready = sem("const_in"), sem("const_ready")
        wk_in = sem("wk_in")
        kept_in, kept_ready, rest_ready = sem("kept_in"), sem("kept_ready"), sem("rest_ready")
        ctx_in, x_in = two("ctx_in"), two("x_in")
        stored = two("stored")
        k_done, k_high, k_rest = sem("k_done"), sem("k_high"), sem("k_rest")
        k_middle, k_split, q_split = sem("k_middle"), sem("k_split"), sem("q_split")
        v_done, v_ready = sem("v_done"), sem("v_ready")
        var_ready, std_ready = sem("var_ready"), sem("std_ready")
        x_normed, x_turned, xt_ready = sem("x_normed"), sem("x_turned"), sem("xt_ready")
        q_done, q_whole, q_high = sem("q_done"), sem("q_whole"), sem("q_high")
        q_rest, q_middle = sem("q_rest"), sem("q_middle")
        dve_step, passed = sem("dve_step1"), sem("passed1")
        block = ctx.enter_context(nc.Block())
        GROUPS = [range(g, min(g + 4, NC)) for g in range(0, NC, 4)]
        NG4 = len(GROUPS)
        CONSTS = 16 * 6
        STORES = 16 * (PARTS + NCOPY + 1)

        @block.gpsimd
        def _(pool):
            for s in range(2):
                pool.sem_inc(stored[s], 16)
            for s in range(2):
                nc.gpsimd.memset(vs[:, s], 1.0).then_inc(const_ready, 1)
            nc.gpsimd.memset(eps[:], EPS).then_inc(const_ready, 1)
            pool.wait_ge(const_in, CONSTS)
            nc.gpsimd.tensor_copy(kept.identb[:], ident[:]).then_inc(kept_ready, 1)

            def low(i, s):
                pool.wait_ge(k_middle, 2 * i + s + 1)
                nc.gpsimd.tensor_tensor(kp[:, s, 2], kr[:, s], kp[:, s, 1], ALU.subtract).then_inc(k_split, 1)

            low(0, 0)
            pool.wait_ge(kept_in, 16 * 6)
            nc.gpsimd.tensor_copy(kept.spread[:], spread_f[:]).then_inc(kept_ready, 1)
            low(0, 1)
            for s in range(SLOTS):
                for t, value in ((operands.kx, 1.0), (operands.qx, 0.0), (operands.qm, 0.0)):
                    nc.gpsimd.memset(t[s][:], value).then_inc(rest_ready, 1)
            with pool.Fori(1, B // 2) as i:
                for s in range(2):
                    low(i, s)

        @block.sync
        def _(sp):
            xs = io["x"].rearrange("b (t p) d -> b p t d", p=P)

            def load_x(n, s):
                sp.dma_start(xin[:, s], xs[bass.ds(n, 1)].rearrange("a p t d -> p (a t) d")).then_inc(x_in[s], 16)

            def load_ctx(n, s):
                sp.dma_start(ctxt[:, s], io["ctxT"][bass.ds(n, 1)].rearrange("a c k -> (a c) k")).then_inc(ctx_in[s], 16)

            load_x(0, 0)
            sp.dma_start(wk[:], io["wkT"]).then_inc(wk_in, 16)
            load_ctx(0, 0)
            for t, name in ((wv, "wvT"), (ident, "ident"), (wq, "wqT")):
                sp.dma_start(t[:], io[name]).then_inc(const_in, 16)
            sp.dma_start(bqk[:, 0:1], io["bq"].rearrange("(d a) -> d a", a=1)).then_inc(const_in, 16)
            sp.dma_start(bqk[:, 1:2], io["bk"].rearrange("(d a) -> d a", a=1)).then_inc(const_in, 16)
            sp.dma_start(bv[:], io["bv"].partition_broadcast(P)).then_inc(const_in, 16)
            load_x(1, 1)
            load_ctx(1, 1)
            for t, name in ((kept.wo, "woT"), (kept.gw, "gate_wT"), (kept.pick, "pick"), (spread_f, "spread")):
                sp.dma_start(t[:], io[name]).then_inc(kept_in, 16)
            sp.dma_start(kept.bo[:], io["bo"].partition_broadcast(P)).then_inc(kept_in, 16)
            sp.dma_start(kept.gb[:], io["gate_bias"].partition_broadcast(P)).then_inc(kept_in, 16)

            def store_k(b, s):
                for part in range(PARTS):
                    sp.wait_ge((k_high, k_middle, k_split)[part], b + 1)
                    sp.dma_start(ke[bass.ds(b, 1), :, part].rearrange("a h r k -> (a h) r k"), kp[:, s, part]).then_inc(stored[s], 16)

            def batch(i, s, first=False, last=False):
                b = 2 * i + s
                if not first:
                    store_k(b - 1, 1 - s)
                if not last:
                    sp.wait_ge(v_done, NG4 * (b + 1) + 1)
                    load_ctx(b + 2, s)
                    sp.wait_ge(x_normed, b + 1)
                    load_x(b + 2, s)
                sp.wait_ge(v_ready, NG4 * (b + 1) + 2)
                sp.dma_start(ve[bass.ds(b, 1)].rearrange("a n p w -> p (a n) w"),
                             vs[:, s].rearrange("p n c w -> p n (c w)")).then_inc(stored[s], 16)
                sp.wait_ge(q_split, b + 1)
                for c, part in enumerate(COPIES_Q):
                    sp.dma_start(qe[bass.ds(b, 1), :, c].rearrange("a h r q -> (a h) r q"), qp[:, s, part]).then_inc(stored[s], 16)

            batch(0, 0, first=True)
            with sp.Fori(0, B // 2 - 2) as i:
                batch(i, 1)
                batch(i + 1, 0)
            batch(B // 2 - 2, 1)
            sp.wait_ge(rest_ready, 3 * SLOTS)
            sp.wait_ge(stored[0], 16 + STORES)
            operands.load(sp, ke, qe, ve, 0, 0)
            batch(B // 2 - 1, 0, last=True)
            batch(B // 2 - 1, 1, last=True)
            store_k(B - 1, 1)
            for s in range(2):
                sp.wait_ge(stored[s], STORES * B // 2 + 16)

        @block.tensor
        def _(pe):
            pe.wait_ge(wk_in, 16)
            pe.sem_inc(v_done, 1)
            with pe.Fori(0, B // 2) as i:
                for s in range(2):
                    n = 2 * i + s
                    pe.wait_ge(ctx_in[s], 16 * (i + 1))
                    pe.wait_ge(k_rest, n + 1)
                    for a in range(0, SK, BANK):
                        w = min(BANK, SK - a)
                        last = nc.tensor.matmul(k_ps[:, a:a + w], wk[:], ctxt[:, s, a:a + w], start=True, stop=True)
                    last.then_inc(k_done, 1)
                    for g, chunks in enumerate(GROUPS):
                        if g == 0 and s == 0:
                            pe.wait_ge(const_in, CONSTS)
                        pe.wait_ge(v_ready, NG4 * n + g + 1)
                        for c in chunks:
                            w = min(P, SK - c * P)
                            last = nc.tensor.matmul(v_ps[g % 2][0:w, c % 4], ctxt[:, s, c * P:c * P + w], wv[:], start=True, stop=True)
                        last.then_inc(v_done, 1)
                        if g == 0:
                            pe.wait_ge(x_normed, n + 1)
                            for t in range(QB):
                                last = nc.tensor.transpose(t_ps[:, t * P:(t + 1) * P], xn[:, s, t], ident[:])
                            last.then_inc(x_turned, 1)
                        if g == 2:
                            pe.wait_ge(xt_ready, n + 1)
                            pe.wait_ge(q_whole, n + 1)
                            nc.tensor.matmul(q_ps, wq[:], xt[:, s], start=True, stop=True).then_inc(q_done, 1)

        @block.scalar
        def _(act):
            act.wait_ge(const_in, CONSTS)
            act.wait_ge(const_ready, 3)
            act.sem_inc(q_whole, 1)
            nc.scalar.mul(bqk[:, 2:3], bqk[:, 0:1], QSCALE).then_inc(const_ready, 1)
            act.wait_ge(const_ready, 4)

            def deviation(n, s):
                act.wait_ge(var_ready, n + 1)
                nc.scalar.activation(rs[:, s], mv[:, s, :, 1], ACT.Sqrt, bias=eps[:]).then_inc(std_ready, 1)

            def batch(i, s, last=False):
                n = 2 * i + s
                act.wait_ge(k_done, n + 1)
                act.wait_ge(stored[s], STORES * i + 16)
                nc.scalar.activation(kp[:, s, 0], k_ps, ACT.Identity, bias=bqk[:, 1:2]).then_inc(k_high, 1)
                act.wait_ge(x_turned, n + 1)
                nc.scalar.copy(xt[:, s], t_ps).then_inc(xt_ready, 1)
                act.wait_ge(k_rest, n + 2)
                nc.scalar.copy(kp[:, s, 1], kr[:, s]).then_inc(k_middle, 1)
                if not last:
                    deviation(n + 1, 1 - s)
                act.wait_ge(q_done, n + 1)
                nc.scalar.activation(qf[:, s], q_ps, ACT.Identity, bias=bqk[:, 2:3], scale=QSCALE).then_inc(q_whole, 1)
                act.wait_ge(q_whole, n + 2)
                nc.scalar.copy(qp[:, s, 0], qf[:, s]).then_inc(q_high, 1)
                act.wait_ge(q_rest, n + 1)
                nc.scalar.copy(qp[:, s, 1], qr[:, s]).then_inc(q_middle, 1)

            deviation(0, 0)
            with act.Fori(0, B // 2 - 1) as i:
                for s in range(2):
                    batch(i, s)
            for s in range(2):
                batch(B // 2 - 1, s, last=s == 1)

        @block.vector
        def _(dve):
            dve.sem_inc(k_rest, 1)
            dve.sem_inc(v_ready, 2)
            PER = QB + 1
            step = Steps(dve, dve_step)

            def norm_a(n, s, uses):
                step.base, step.n = PER * n, 0
                dve.wait_ge(x_in[s], 16 * (uses + 1))
                for t in range(QB):
                    step.mark(nc.vector.bn_stats(st[:, s, t], xin[:, s, t]))
                step.wait_apart(passed)
                for t in range(QB):
                    last = nc.vector.bn_aggr(mv[:, s, t], st[:, s, t])
                last.then_inc(var_ready, 1)

            def norm_b(n, s):
                dve.wait_ge(std_ready, n + 1)
                step.mark(nc.vector.reciprocal(rr[:, s], rs[:, s]))
                step.wait()
                for t in range(QB):
                    last = nc.vector.tensor_scalar(xn[:, s, t], xin[:, s, t], mv[:, s, t, 0:1], rr[:, s, t:t + 1], ALU.subtract, ALU.mult)
                last.then_inc(x_normed, 1)

            def values(n, s, g):
                dve.wait_ge(v_done, NG4 * n + g + 2)
                chunks = GROUPS[g]
                w = P if g < NG4 - 1 else LAST
                for h in range(2):
                    out = vs[0:w, s, :, chunks[0]:chunks[-1] + 1, (DH + 1) * h:(DH + 1) * h + DH].rearrange("p n c d -> p c n d")
                    src = v_ps[g % 2][0:w, 0:len(chunks)].rearrange("p c (n h d) -> p c n h d", h=2, d=DH)[:, :, :, h]
                    bias = bv[0:w].rearrange("p (n h d) -> p n h d", h=2, d=DH)[:, :, h].unsqueeze(1).broadcast_to([w, len(chunks), PAIRS, DH])
                    ins = nc.vector.tensor_tensor(out, src, bias, ALU.add)
                ins.then_inc(v_ready, 1)

            def batch(i, s, last=False):
                n = 2 * i + s
                dve.wait_ge(stored[s], STORES * i + 16)
                values(n, s, 0)
                values(n, s, 1)
                dve.wait_ge(k_high, n + 1)
                nc.vector.scalar_tensor_tensor(kr[:, s], k_ps, bqk[:, 1:2], kp[:, s, 0], ALU.add, ALU.subtract).then_inc(k_rest, 1)
                if not last:
                    norm_a(n + 1, 1 - s, i + s)
                values(n, s, 2)
                values(n, s, 3)
                dve.wait_ge(q_high, n + 1)
                nc.vector.tensor_tensor(qr[:, s], qf[:, s], qp[:, s, 0], ALU.subtract).then_inc(q_rest, 1)
                if not last:
                    norm_b(n + 1, 1 - s)
                dve.wait_ge(q_middle, n + 1)
                nc.vector.tensor_tensor(qp[:, s, 2], qr[:, s], qp[:, s, 1], ALU.subtract).then_inc(q_split, 1)

            norm_a(0, 0, 0)
            norm_b(0, 0)
            dve.wait_ge(const_in, CONSTS)
            dve.wait_ge(const_ready, 4)
            with dve.Fori(0, B // 2 - 1) as i:
                for s in range(2):
                    batch(i, s)
            for s in range(2):
                batch(B // 2 - 1, s, last=s == 1)


def attend(nc, io, ke, qe, ve, kept, operands, att, wh, wl):
    with ExitStack() as ctx:
        sb = lambda name, shape, dt=F32: ctx.enter_context(nc.sbuf_tensor(name, shape, dt))
        sem = lambda name: ctx.enter_context(nc.semaphore(name))
        slots = lambda name: [sem(f"{name}{s}") for s in range(SLOTS)]

        identb, pick = kept.identb, kept.pick
        kx, qx, qm, vx, loaded = operands.kx, operands.qx, operands.qm, operands.vx, operands.loaded
        prob = [sb(f"prob{s}", [P, NC, 2 * SQ]) for s in range(2)]
        part_max = sb("part_max", [P, 2, 4, QUARTERS])
        neg, neg_rest = sb("neg", [P, 2, 4]), sb("neg_rest", [P, 2, 4])
        neg_parts = sb("neg_parts", [P, 2, 4, 3], BF16)
        neg_rows = [sb(f"neg_rows{s}", [3, 4 * P], BF16) for s in range(2)]
        ev = [sb(f"ev{s}", [P, 2 * SQ]) for s in range(PAIRS)]
        sums, inverse = sb("sums", [P, 2 * SQ]), sb("inverse", [P, SQ])
        w_all = sb("w_all", [P, PIECES * PIECE])
        ps = ctx.enter_context(nc.psum_tensor("ps2", [P, 8 * BANK], F32))
        s_ps = [ps[:, n * BANK:(n + 1) * BANK] for n in range(3)]
        m_ps = [ps[:, n * BANK:(n + 1) * BANK] for n in range(3, 6)]
        o_ps = ps[:, 6 * BANK:7 * BANK]
        w_ps = ps[:, 7 * BANK:8 * BANK]
        t_ps = [s_ps[n][:, 0:2 * P].bitcast(BF16)[0:3] for n in range(3)]

        const_ready = sem("const_ready2")
        w_in = sem("w_in")
        pair_done, neg_stored = slots("pair_done"), slots("neg_stored")
        max_scored, max_reduced = sem("max_scored"), sem("max_reduced")
        neg_ready, neg_split = sem("neg_ready"), sem("neg_split")
        scored, exped = sem("scored"), sem("exped")
        evacuated, picked, normalised = sem("evacuated"), sem("picked"), sem("normalised")
        sums_copied, inverted, pool_step, passed = sem("sums_copied"), sem("inverted"), sem("pool_step2"), sem("passed2")
        block = ctx.enter_context(nc.Block())
        MU = 4 * QUARTERS
        TURN = 7
        USES = NC + 1
        BODY = PAIRS * USES
        LOOPS = B - 1
        EVAC = 1
        WEIGHS = NC // CT + 1

        def of(i, t):
            return PAIRS * i + t, t % SLOTS, PAIRS // SLOTS * i + t // SLOTS

        def use(c):
            return c + (c >= TURN)

        def ring(x, body):
            return x % 3, x - 3 if x >= 3 else max(y for y in range(body) if y % 3 == x) - body

        @block.gpsimd
        def _(pool):
            for t in range(PAIRS - 1):
                ins = nc.gpsimd.memset(ev[t][:], 1.0)
            ins.then_inc(const_ready, 1)
            nc.gpsimd.memset(w_all[:, 3 * ALL * P:], 0.0).then_inc(const_ready, 1)

            def split(i, t, step):
                n, _, _ = of(i, t)
                a = t % 2
                pool.wait_ge(neg_ready, n + 1)
                pool.sem_inc(passed, 1)
                step.mark(nc.gpsimd.tensor_copy(neg_parts[:, a, :, 0], neg[:, a]))
                step.wait()
                step.mark(nc.gpsimd.tensor_tensor(neg_rest[:, a], neg[:, a], neg_parts[:, a, :, 0], ALU.subtract))
                step.wait_apart(passed)
                step.mark(nc.gpsimd.tensor_copy(neg_parts[:, a, :, 1], neg_rest[:, a]))
                step.wait()
                nc.gpsimd.tensor_tensor(neg_parts[:, a, :, 2], neg_rest[:, a], neg_parts[:, a, :, 1], ALU.subtract).then_inc(neg_split, 1)

            def normalise(i):
                pool.wait_ge(inverted, 4 * i + 4)
                nc.gpsimd.tensor_tensor(att[:, bass.ds(i, 1)].rearrange("p a q -> p (a q)"),
                                        sums[:, 0:SQ], inverse[:], ALU.mult).then_inc(normalised, 1)

            pool.sem_inc(normalised, 1)
            first = Steps(pool, pool_step)
            split(0, 0, first)
            split(0, 1, first)
            PER = 3 * PAIRS + 1
            pool.wait_ge(w_in, 16 * 7)
            pool.wait_ge(const_ready, 3)
            with pool.Fori(0, LOOPS) as i:
                step = Steps(pool, pool_step, 6 + PER * i)
                for t in range(PAIRS):
                    split(i, t + 2, step)
                    if t == 0:
                        at = bass.ds(i * PIECE, PIECE)
                        step.mark(nc.gpsimd.tensor_copy(wh[:, at], w_all[:, at]))
                    if t == 1:
                        step.wait()
                        nc.gpsimd.tensor_tensor(wl[:, at], w_all[:, at], wh[:, at].bitcast(F32), ALU.subtract)
                normalise(i)
            i = LOOPS
            step = Steps(pool, pool_step, 6 + PER * i)
            for t in range(PAIRS - 2):
                split(i, t + 2, step)
            normalise(i)
            normalise(i + 1)

        @block.sync
        def _(sp):
            def load(i, t):
                n, s, uses = of(i, t)
                sp.wait_ge(pair_done[s], uses + 1)
                operands.load(sp, ke, qe, ve, n, s)

            def store_neg(i, t, first=False):
                n, s, uses = of(i, t)
                if first:
                    sp.wait_ge(exped, 3)
                else:
                    sp.wait_ge(exped, USES * (n - 1) + TURN + 1 + 3)
                for h in range(2):
                    sp.dma_start(qx[s][64 * h + ROWS:64 * h + ROWS + 3, SQ * h:SQ * h + SQ],
                                 neg_rows[t % 2][:, SQ * h:SQ * h + SQ]).then_inc(neg_stored[s], 16)

            for n in (1, 2):
                operands.load(sp, ke, qe, ve, n, n)
            for k, (name, shared) in enumerate((("w_gateT", "sh_gateT"), ("w_upT", "sh_upT"), ("w_downT", "sh_downT"))):
                sp.dma_start(w_all[:, k * ALL * P:(k * ALL + UNITS) * P], io[name]).then_inc(w_in, 16)
                sp.dma_start(w_all[:, (k * ALL + UNITS) * P:(k + 1) * ALL * P], io[shared]).then_inc(w_in, 16)
            sp.dma_start(kept.xin[:], io["x"].rearrange("b (t p) d -> p (b t) d", p=P)[:, 0:TT]).then_inc(w_in, 16)
            store_neg(0, 0, first=True)
            with sp.Fori(0, LOOPS) as i:
                for t in range(PAIRS):
                    load(i, t + 3)
                    store_neg(i, t + 1)
            i = LOOPS
            for t in range(PAIRS - 1):
                if t + 3 < PAIRS:
                    load(i, t + 3)
                store_neg(i, t + 1)

        @block.tensor
        def _(pe):
            for s in range(SLOTS):
                pe.sem_inc(pair_done[s], 1)

            def max_unit(i, t, u, prologue=False):
                n, s, uses = of(i, t)
                x = MU * (t if prologue else t - 2) + u
                bank, before = ring(x + (MU * (PAIRS - 2) if prologue else 0), MU * PAIRS)
                if u == 0:
                    pe.wait_ge(loaded[s], 16 * 9 * (uses + 1))
                if not prologue:
                    pe.wait_ge(max_reduced, 2 * MU + MU * PAIRS * i + before + 1)
                elif x >= 3:
                    pe.wait_ge(max_reduced, x - 2)
                a, w = KEYS_OF[u % QUARTERS]
                q = u // QUARTERS
                nc.tensor.matmul(m_ps[bank][:, 0:w], qm[s][:, q * P:(q + 1) * P], kx[s][:, a:a + w],
                                 start=True, stop=True).then_inc(max_scored, 1)

            def turn_neg(i, t, first=False, none=False):
                n, _, _ = of(i, t)
                bank, before = ring(USES * (t - 1) + TURN, BODY) if not first else (0, None)
                if not first:
                    pe.wait_ge(exped, BODY * i + before + 1 + 3)
                if not none:
                    pe.wait_ge(neg_split, n + 1)
                for u in range(4):
                    last = nc.tensor.transpose(t_ps[bank][:, u * P:(u + 1) * P], neg_parts[:, t % 2, u], identb[:])
                last.then_inc(scored, 1)

            def score(i, t, c):
                n, s, uses = of(i, t)
                bank, before = ring(USES * t + use(c), BODY)
                if c == 0:
                    pe.wait_ge(neg_stored[s], 16 * 2 * (uses + 1))
                pe.wait_ge(exped, BODY * i + before + 1 + 3)
                w = P if c < NC - 1 else LAST
                nc.tensor.matmul(s_ps[bank][0:w, :], kx[s][:, c * P:c * P + w], qx[s][:, :], start=True, stop=True).then_inc(scored, 1)

            def weigh(i, t, g):
                n, s, uses = of(i, t)
                if g == 0:
                    pe.wait_ge(evacuated, n + 1)
                for j in range(CT):
                    c = min(CT * g + j, NC - 1)
                    if c < NC - 1 or j == 0:
                        pe.wait_ge(exped, BODY * i + USES * t + use(c) + 1 + 3)
                    w, cols = (P, slice(0, 2 * SQ)) if c < NC - 1 else (LAST, slice(j * P, (j + 1) * P))
                    last = nc.tensor.matmul(o_ps[VW * j:VW * j + VC, cols], vx[s][0:w, c * VC:(c + 1) * VC], prob[t % 2][0:w, c, cols],
                                            start=g == 0, stop=c == NC - 1, skip_group_check=True)
                if g == WEIGHS - 1:
                    last.then_inc(pair_done[s], 1)

            def pick_out(i, t, before=False):
                n, _, _ = of(i, t)
                half, ones, h = 1 - t // CT % 2, t % CT // 2, t % 2
                if t % CT == 0 and not before:
                    pe.wait_ge(evacuated, n + 1)
                if t == CT and not before:
                    pe.wait_ge(sums_copied, i + 1)
                for j in range(CT):
                    last = nc.tensor.matmul(w_ps[VW * j:VW * (j + 1), ones * SQ:(ones + 1) * SQ],
                                            pick[:, ones, 2 * half + h], ev[CT * half + j][:, h * SQ:(h + 1) * SQ],
                                            start=t == CT, stop=t % PAIRS == CT - 1, skip_group_check=True)
                if t % CT == CT - 1:
                    last.then_inc(picked, 1)

            ORDER = "SMMSSSMMOMSMSMSWTMSMMSSMSMWMSMSMMWW"

            def pair(i, t, turn=True, ahead=True):
                c = u = k = 0
                for what in ORDER:
                    if what == "S":
                        score(i, t, c)
                        c += 1
                    elif what == "M":
                        if ahead:
                            max_unit(i, t + 2, u)
                        u += 1
                    elif what == "W":
                        weigh(i, t, k)
                        k += 1
                    elif what == "O":
                        pick_out(i, t)
                    else:
                        assert c == TURN
                        turn_neg(i, t + 1, none=not turn)
                assert (c, u, k) == (NC, MU, WEIGHS)

            for t in range(2):
                for u in range(MU):
                    max_unit(0, t, u, prologue=True)
                    if t == 1 and u == MU // 2:
                        turn_neg(0, 0, first=True)
            pe.wait_ge(const_ready, 3)
            for t in range(CT, PAIRS):
                pick_out(-1, t, before=True)
            with pe.Fori(0, LOOPS) as i:
                for t in range(PAIRS):
                    pair(i, t)
            i = LOOPS
            for t in range(PAIRS):
                pair(i, t, turn=t + 1 < PAIRS, ahead=t + 2 < PAIRS)
            for t in range(CT):
                pick_out(i, PAIRS + t)

        @block.scalar
        def _(act):
            act.sem_inc(exped, 2)

            def copy_neg(i, t, first=False):
                n, _, _ = of(i, t)
                act.wait_ge(scored, 1 if first else USES * (n - 1) + TURN + 2)
                bank, _ = ring(USES * (t - 1) + TURN, BODY) if not first else (0, None)
                nc.scalar.copy(neg_rows[t % 2][:], t_ps[bank]).then_inc(exped, 1)

            def evacuate(i, t):
                _, s, uses = of(i, t - 1)
                act.wait_ge(pair_done[s], uses + 2)
                if t == 1:
                    act.wait_ge(picked, 2 * i + 1)
                if t == CT + 1:
                    act.wait_ge(picked, 2 * i + 2)
                nc.scalar.copy(ev[(t - 1) % PAIRS][:], o_ps).then_inc(evacuated, 1)

            def copy_sums(i):
                act.wait_ge(picked, 2 * i + 2)
                act.wait_ge(normalised, i + 1)
                nc.scalar.copy(sums[:], w_ps).then_inc(sums_copied, 1)

            def pair(i, t):
                n, s, uses = of(i, t)
                for c in range(NC):
                    if c == EVAC:
                        evacuate(i, t)
                    if c == TURN:
                        copy_neg(i, t + 1)
                    if c == NC - 3 and t == CT - 1:
                        copy_sums(i)
                    act.wait_ge(scored, USES * n + use(c) + 2)
                    w = P if c < NC - 1 else LAST
                    bank, _ = ring(USES * t + use(c), BODY)
                    nc.scalar.activation(prob[t % 2][0:w, c], s_ps[bank][0:w, :], ACT.Exp).then_inc(exped, 1)

            copy_neg(0, 0, first=True)
            act.wait_ge(const_ready, 3)
            with act.Fori(0, LOOPS) as i:
                for t in range(PAIRS):
                    pair(i, t)
            i = LOOPS
            for t in range(PAIRS):
                pair(i, t)
            evacuate(i, PAIRS)
            copy_sums(i + 1)

        @block.vector
        def _(dve):

            def reduce_unit(i, t, u, prologue=False):
                n, _, _ = of(i, t)
                x = MU * (t + PAIRS - 2 if prologue else t - 2) + u
                bank, _ = ring(x, MU * PAIRS)
                q, k = u // QUARTERS, u % QUARTERS
                dve.wait_ge(max_scored, MU * n + u + 1)
                nc.vector.tensor_reduce(part_max[:, t % 2, q, k:k + 1], m_ps[bank][:, 0:KEYS_OF[k][1]],
                                        AX.X, ALU.max).then_inc(max_reduced, 1)

            def negate(i, t):
                n, _, _ = of(i, t)
                dve.wait_ge(max_reduced, MU * (n + 1))
                nc.vector.tensor_reduce(neg[:, t % 2], part_max[:, t % 2], AX.X, ALU.max, negate=True).then_inc(neg_ready, 1)

            def invert(i, k):
                if k == 0:
                    dve.wait_ge(sums_copied, i + 1)
                cols = slice(k * SQ // 4, (k + 1) * SQ // 4)
                nc.vector.reciprocal(inverse[:, cols], sums[:, SQ:2 * SQ][:, cols]).then_inc(inverted, 1)

            def pair(i, t, ahead=True):
                for u in range(MU):
                    if ahead:
                        reduce_unit(i, t + 2, u)
                    if t >= CT and u == MU // 2:
                        invert(i, t - CT)
                if ahead:
                    negate(i, t + 2)

            for t in range(2):
                for u in range(MU):
                    reduce_unit(0, t, u, prologue=True)
                negate(0, t)
            nc.vector.memset(o_ps, 1.0).then_inc(const_ready, 1)
            with dve.Fori(0, LOOPS) as i:
                for t in range(PAIRS):
                    pair(i, t)
            i = LOOPS
            for t in range(PAIRS):
                pair(i, t, ahead=t + 2 < PAIRS)
            for k in range(4):
                invert(i + 1, k)


def mix(nc, io, kept, att, wh, wl, out):
    with ExitStack() as ctx:
        sb = lambda name, shape, dt=F32: ctx.enter_context(nc.sbuf_tensor(name, shape, dt))
        sem = lambda name: ctx.enter_context(nc.semaphore(name))

        ident, identb, wo, gw, bo, gb = kept.ident, kept.identb, kept.wo, kept.gw, kept.bo, kept.gb
        eps, spread, xin = kept.eps, kept.spread, kept.xin
        part = lambda w, k, j: w[:, (k * ALL + j) * P:(k * ALL + j + 1) * P]
        x1 = [sb(f"x1{s}", [P, TT, D]) for s in range(2)]
        hf = sb("hf", [P, TB])
        hh = [sb(f"hh{s}", [P, TB], F32R) for s in range(2)]
        hl = [sb(f"hl{s}", [P, TB], F32R) for s in range(2)]
        ct = [sb(f"ct{s}", [3 * NE, TB], BF16) for s in range(2)]
        ot = sb("ot", [P, TB])
        st, mv, rs = sb("st3", [P, TT, 6]), sb("mv3", [P, TT, 2]), sb("rs3", [P, TT])
        hn = sb("hn", [P, TT, D])
        score = sb("score", [P, TT, NE])
        biased, masked, left = sb("biased", [P, TT, NE]), sb("masked", [P, TT, NE]), sb("left", [P, TT, NE])
        hi, lo = sb("hi", [P, TT * NG, 2]), sb("lo", [P, TT * NG, 2])
        top, second = sb("top", [P, TT * NG]), sb("second", [P, TT * NG])
        gscore, gleft = sb("gscore", [P, TT, NG]), sb("gleft", [P, TT, NG])
        best = sb("best", [P, TT, 8])
        total = sb("total", [P, TT])
        cw, cr = sb("cw", [P, TT, NE]), sb("cr", [P, TT, NE])
        cp = sb("cp", [P, TT, 3, NE], BF16)
        sg = [sb(f"sg{n}", [P, TB]) for n in range(2)]
        gu = [sb(f"gu{n}", [P, TB]) for n in range(2)]
        hid = [sb(f"hid{n}", [P, TB]) for n in range(2)]
        hid_hi = [sb(f"hid_hi{n}", [P, TB], F32R) for n in range(2)]
        hid_lo = [sb(f"hid_lo{n}", [P, TB], F32R) for n in range(2)]
        yt = sb("yt", [P, TB])
        y = sb("y", [P, TT, D])
        ps = ctx.enter_context(nc.psum_tensor("ps3", [P, 8 * BANK], F32))
        bank = lambda n: ps[:, n * BANK:(n + 1) * BANK]
        g_ps, u_ps, c_ps = [bank(0), bank(1)], [bank(2), bank(3)], [bank(4), bank(5)]
        y_ps = bank(6)
        z_ps = bank(7)
        z_tiles = z_ps.rearrange("p (t d) -> p t d", t=TT)
        z_bf = z_ps.bitcast(BF16)[0:3 * NE, 0:TB]

        x_in, x_biased, ob_ready = sem("x_in3"), sem("x_biased"), sem("ob_ready")
        pe_stage, act_stage, dve_stage = sem("pe_stage"), sem("act_stage"), sem("dve_stage")
        gated, up, spreaded = sem("gated"), sem("up"), sem("spreaded")
        silued, multiplied, weighted = sem("silued"), sem("multiplied"), sem("weighted")
        hi_ready, lo_ready, downed = sem("hi_ready"), sem("lo_ready"), sem("downed")
        y_copied, y_turned = sem("y_copied"), sem("y_turned")
        y_ready, y_stored = sem("y_ready"), sem("y_stored")
        dve_step, passed, gathers = sem("dve_step3"), sem("passed3"), sem("gathers")
        block = ctx.enter_context(nc.Block())
        PE_ST, ACT_ST, DVE_ST = 4, 5, 5
        STEPS = 43


        def blocks(eng, prepare, expert_block):
            for k in range(ALL):
                prepare(0, 0, k)
            expert_block(0, 0, lambda k: prepare(1, 1, k), first=True)
            with eng.Fori(0, NBLK // 2 - 1) as i:
                for s in (1, 0):
                    n = 2 * i + 2 - s
                    expert_block(n, s, lambda k: prepare(n + 1, 1 - s, k))
            expert_block(NBLK - 1, 1, lambda k: None)

        @block.gpsimd
        def _(pool):
            pool.sem_inc(x_in, 16)
            pool.sem_inc(lo_ready, 2)

            def prepare(n, s, k):
                if k == 0:
                    if type(n) is not int or n > 0:
                        pool.wait_ge(pe_stage, PE_ST * n - PE_ST + 1)
                        pool.sem_inc(gathers, 1)
                    nc.gpsimd.tensor_copy(ot[:].rearrange("p (b q) -> p b q", q=SQ),
                                          att[:, bass.ds(1 + n * (TB // SQ), TB // SQ)]).then_inc(ob_ready, 1)
                elif k == 1:
                    pool.wait_ge(x_in, 16 * (n + 1))
                    nc.gpsimd.tensor_tensor(xin[:], xin[:], bo[:].unsqueeze(1).broadcast_to([P, TT, D]), ALU.add).then_inc(x_biased, 1)

            def low(m, a):
                pool.wait_ge(hi_ready, m + 1)
                nc.gpsimd.tensor_tensor(hid_lo[a][:], hid[a][:], hid_hi[a][:].bitcast(F32), ALU.subtract).then_inc(lo_ready, 1)

            def expert_block(n, s, stage, first=False):
                for j in range(ALL):
                    if j or not first:
                        low(ALL * n + j - 1, (s + j - 1) % 2)
                    stage(j)

            blocks(pool, prepare, expert_block)
            low(ALL * NBLK - 1, (ALL * NBLK - 1) % 2)

        @block.sync
        def _(sp):
            xt = io["x"].rearrange("b (t p) d -> p (b t) d", p=P)
            ot_ = out.rearrange("b (t p) d -> p (b t) d", p=P)
            def store(n):
                sp.wait_ge(y_ready, n + 3)
                sp.dma_start(ot_[:, bass.ds(TT * n, TT)], y[:]).then_inc(y_stored, 16)

            def load(n):
                sp.wait_ge(dve_stage, DVE_ST * (n - 1) + 1)
                sp.dma_start(xin[:], xt[:, bass.ds(TT * n, TT)]).then_inc(x_in, 16)

            load(1)
            load(2)
            with sp.Fori(0, NBLK - 3) as n:
                store(n)
                load(n + 3)
            for n in range(NBLK - 3, NBLK):
                store(n)
            sp.wait_ge(y_stored, 16 * NBLK + 16)

        @block.tensor
        def _(pe):

            pe.sem_inc(downed, 2)

            def prepare(n, s, k):
                if k == 3:
                    pe.wait_ge(ob_ready, n + 1)
                    pe.wait_ge(y_ready, n + 1)
                    for t in range(TT):
                        last = nc.tensor.matmul(z_tiles[:, t], ot[:, t * P:(t + 1) * P], wo[:], start=True, stop=True)
                elif k == 6:
                    pe.wait_ge(dve_stage, DVE_ST * n + 3)
                    for t in range(TT):
                        last = nc.tensor.transpose(z_tiles[:, t], hn[:, t], ident[:])
                elif k == 8:
                    pe.wait_ge(act_stage, ACT_ST * n + 3)
                    for t in range(TT):
                        last = nc.tensor.matmul(z_ps[:, t * NE:(t + 1) * NE], hf[:, t * P:(t + 1) * P], gw[:], start=True, stop=True)
                elif k == 16:
                    pe.wait_ge(dve_stage, DVE_ST * n + 5)
                    for t in range(TT):
                        last = nc.tensor.transpose(z_bf[:, t * P:(t + 1) * P], cp[:, t].rearrange("p c e -> p (c e)"), identb[:])
                else:
                    return
                last.then_inc(pe_stage, 1)

            def product(out, k, j, hi, lo, start, stop, lo_count=None):
                for w, x in ((wh, hi), (wl, hi), (wh, lo)):
                    if x is lo and lo_count is not None:
                        pe.wait_ge(lo_ready, lo_count)
                    last = nc.tensor.matmul(out, part(w, k, j), x[:], start=start and w is wh and x is hi,
                                            stop=stop and x is lo, skip_group_check=True)
                return last

            def down(n, j, a):
                if j == 0:
                    pe.wait_ge(y_copied, n + 1)
                pe.wait_ge(hi_ready, ALL * n + j + 1)
                last = product(y_ps, 2, j, hid_hi[a], hid_lo[a], j == 0, j == ALL - 1, lo_count=ALL * n + j + 3)
                last.then_inc(downed, 1)

            def turn_y(n):
                pe.wait_ge(y_copied, n + 2)
                for t in range(TT):
                    last = nc.tensor.transpose(z_tiles[:, t], yt[:, t * P:(t + 1) * P], ident[:])
                last.then_inc(y_turned, 1)

            def expert_block(n, s, stage, first=False):
                for j in range(ALL):
                    a, m = (s + j) % 2, ALL * n + j
                    if j == 0:
                        pe.wait_ge(dve_stage, DVE_ST * n + 5)
                    pe.wait_ge(silued, m + 1)
                    product(g_ps[a], 0, j, hh[s], hl[s], True, True).then_inc(gated, 1)
                    pe.wait_ge(weighted, m + 1)
                    product(u_ps[a], 1, j, hh[s], hl[s], True, True).then_inc(up, 1)
                    if j == 0:
                        pe.wait_ge(act_stage, ACT_ST * (n + 1))
                    if j < UNITS:
                        nc.tensor.matmul(c_ps[a], spread[:, j], ct[s][:], start=True, stop=True).then_inc(spreaded, 1)
                    if j == 2 and not first:
                        turn_y(n - 1)
                    if j != 6:
                        stage(j)
                    if j >= 2:
                        down(n, j - 2, a)
                    elif not first:
                        down(n - 1, ALL + j - 2, a)
                    if j == 6:
                        stage(j)

            blocks(pe, prepare, expert_block)
            for j in (ALL - 2, ALL - 1):
                down(NBLK - 1, j, (1 + j) % 2)
            turn_y(NBLK - 1)

        @block.scalar
        def _(act):

            def prepare(n, s, k):
                if k == 5:
                    act.wait_ge(dve_stage, DVE_ST * n + 2)
                    ins = nc.scalar.activation(rs[:], mv[:, :, 1], ACT.Sqrt, bias=eps[:])
                elif k == 7:
                    act.wait_ge(pe_stage, PE_ST * n + 2)
                    nc.scalar.copy(hf[:], z_ps).then_inc(act_stage, 1)
                    ins = nc.scalar.copy(hh[s][:], z_ps)
                elif k == 8:
                    act.wait_ge(pe_stage, PE_ST * n + 3)
                    ins = nc.scalar.activation(score[:].rearrange("p t e -> p (t e)"), z_ps[:, 0:TT * NE], ACT.Exp, scale=-1.0)
                elif k == 16:
                    act.wait_ge(pe_stage, PE_ST * n + 4)
                    ins = nc.scalar.copy(ct[s][:], z_bf)
                else:
                    return
                ins.then_inc(act_stage, 1)

            def copy_y(n):
                act.wait_ge(downed, ALL * (n + 1) + 2)
                nc.scalar.copy(yt[:], y_ps).then_inc(y_copied, 1)

            def high(m, a):
                act.wait_ge(weighted, m + 3)
                act.wait_ge(downed, m + 1)
                nc.scalar.copy(hid_hi[a][:], hid[a][:]).then_inc(hi_ready, 1)

            def expert_block(n, s, stage, first=False):
                for j in range(ALL):
                    a, m = (s + j) % 2, ALL * n + j
                    if j == 2 and not first:
                        copy_y(n - 1)
                    act.wait_ge(gated, m + 1)
                    act.wait_ge(weighted, m + 1)
                    nc.scalar.activation(sg[a][:], g_ps[a], ACT.Silu).then_inc(silued, 1)
                    if j or not first:
                        high(m - 1, 1 - a)
                    stage(j)

            act.sem_inc(silued, 2)
            act.sem_inc(y_copied, 1)
            blocks(act, prepare, expert_block)
            high(ALL * NBLK - 1, (ALL * NBLK - 1) % 2)
            copy_y(NBLK - 1)

        @block.vector
        def _(dve):

            step = Steps(dve, dve_step)

            def prepare(n, s, k):
                    flat = lambda t: t[:].rearrange("p t e -> p (t e)")
                    if k == 3:
                        step.base, step.n = STEPS * n, 0
                        dve.wait_ge(x_biased, n + 1)
                        dve.wait_ge(pe_stage, PE_ST * n + 1)
                        nc.vector.tensor_tensor(x1[s][:], z_tiles, xin[:], ALU.add).then_inc(dve_stage, 1)
                        dve.wait_ge(dve_stage, DVE_ST * n + 1)
                        for t in range(TT):
                            step.mark(nc.vector.bn_stats(st[:, t], x1[s][:, t]))
                        step.wait_apart(passed)
                        for t in range(TT):
                            last = nc.vector.bn_aggr(mv[:, t], st[:, t])
                        last.then_inc(dve_stage, 1)
                    elif k == 5:
                        dve.wait_ge(act_stage, ACT_ST * n + 1)
                        step.mark(nc.vector.reciprocal(rs[:], rs[:]))
                        step.wait()
                        for t in range(TT):
                            last = nc.vector.tensor_scalar(hn[:, t], x1[s][:, t], mv[:, t, 0:1], rs[:, t:t + 1], ALU.subtract, ALU.mult)
                        last.then_inc(dve_stage, 1)
                    elif k == 8:
                        dve.wait_ge(act_stage, ACT_ST * n + 3)
                        nc.vector.tensor_tensor(hl[s][:], hf[:], hh[s][:].bitcast(F32), ALU.subtract).then_inc(dve_stage, 1)
                    elif k == 9:
                        dve.wait_ge(act_stage, ACT_ST * n + 4)
                        step.mark(nc.vector.tensor_scalar(score[:], score[:], 1.0, None, ALU.add))
                        step.wait()
                        step.mark(nc.vector.reciprocal(score[:], score[:]))
                        step.wait()
                        step.mark(nc.vector.tensor_tensor(biased[:], score[:], gb[:].unsqueeze(1).broadcast_to([P, TT, NE]), ALU.add))
                    elif k == 10:
                        step.wait()
                        four = flat(biased).rearrange("p (g a b) -> p g a b", a=2, b=2)
                        step.mark(nc.vector.tensor_tensor(hi[:], four[:, :, :, 0], four[:, :, :, 1], ALU.max))
                        step.mark(nc.vector.tensor_tensor(lo[:], four[:, :, :, 0], four[:, :, :, 1], ALU.min))
                        step.wait()
                        step.mark(nc.vector.tensor_tensor(top[:], hi[:, :, 0], hi[:, :, 1], ALU.max))
                        step.mark(nc.vector.tensor_tensor(second[:], hi[:, :, 0], hi[:, :, 1], ALU.min))
                        step.mark(nc.vector.tensor_tensor(lo[:, :, 0], lo[:, :, 0], lo[:, :, 1], ALU.max))
                        step.wait()
                        step.mark(nc.vector.tensor_tensor(second[:], second[:], lo[:, :, 0], ALU.max))
                        step.wait()
                        step.mark(nc.vector.tensor_tensor(flat(gscore), top[:], second[:], ALU.add))
                    elif k == 11:
                        step.wait_apart(passed)
                        for t in range(TT):
                            step.mark(nc.vector.max(best[:, t], gscore[:, t]))
                        step.wait()
                        step.mark(nc.vector.memset(best[:, :, TOPG:8], UNMATCHED))
                        step.wait_apart(passed)
                        for t in range(TT):
                            step.mark(nc.vector.match_replace(gleft[:, t], best[:, t], gscore[:, t], REPLACED))
                    elif k == 12:
                        step.wait()
                        step.mark(nc.vector.tensor_tensor(gleft[:], gleft[:], gscore[:], ALU.is_lt))
                        step.wait()
                        step.mark(nc.vector.tensor_tensor(flat(masked).rearrange("p (g e) -> p g e", e=NE // NG),
                                                          flat(biased).rearrange("p (g e) -> p g e", e=NE // NG),
                                                          flat(gleft).unsqueeze(2).broadcast_to([P, TT * NG, NE // NG]), ALU.mult))
                        step.wait_apart(passed)
                        for t in range(TT):
                            step.mark(nc.vector.max(best[:, t], masked[:, t]))
                    elif k == 13:
                        step.wait_apart(passed)
                        for t in range(TT):
                            step.mark(nc.vector.match_replace(left[:, t], best[:, t], masked[:, t], REPLACED))
                        step.wait()
                        step.mark(nc.vector.tensor_tensor(left[:], left[:], masked[:], ALU.is_lt))
                        step.wait()
                        step.mark(nc.vector.tensor_tensor(cw[:], score[:], left[:], ALU.mult))
                    elif k == 14:
                        step.wait()
                        step.mark(nc.vector.tensor_reduce(total[:], cw[:], AX.X, ALU.add))
                        step.wait()
                        step.mark(nc.vector.tensor_scalar(total[:], total[:], 1e-20, None, ALU.add))
                        step.wait()
                        step.mark(nc.vector.reciprocal(total[:], total[:]))
                        step.wait()
                        step.mark(nc.vector.scalar_tensor_tensor(cw[:], cw[:], SCALE, total[:].unsqueeze(2).broadcast_to([P, TT, NE]), ALU.mult, ALU.mult))
                        step.wait()
                        step.mark(nc.vector.tensor_copy(cp[:, :, 0], cw[:]))
                        step.wait()
                        step.mark(nc.vector.tensor_tensor(cr[:], cw[:], cp[:, :, 0], ALU.subtract))
                        step.wait()
                        step.mark(nc.vector.tensor_copy(cp[:, :, 1], cr[:]))
                        step.wait()
                        nc.vector.tensor_tensor(cp[:, :, 2], cr[:], cp[:, :, 1], ALU.subtract).then_inc(dve_stage, 1)
                        assert step.n == STEPS

            def add_y(n, s):
                dve.wait_ge(y_turned, n + 1)
                dve.wait_ge(y_stored, 16 * n + 16)
                nc.vector.tensor_tensor(y[:], z_tiles, x1[s][:], ALU.add).then_inc(y_ready, 1)

            def expert_block(n, s, stage, first=False):
                for j in range(ALL):
                    a, m = (s + j) % 2, ALL * n + j
                    dve.wait_ge(silued, m + 3)
                    dve.wait_ge(up, m + 1)
                    if j < UNITS:
                        nc.vector.tensor_tensor(gu[a][:], sg[a][:], u_ps[a], ALU.mult).then_inc(multiplied, 1)
                        dve.wait_ge(lo_ready, m + 1)
                        dve.wait_ge(multiplied, UNITS * n + j + 1)
                        dve.wait_ge(spreaded, UNITS * n + j + 1)
                        nc.vector.tensor_tensor(hid[a][:], gu[a][:], c_ps[a], ALU.mult).then_inc(weighted, 1)
                    else:
                        dve.wait_ge(lo_ready, m + 1)
                        nc.vector.tensor_tensor(hid[a][:], sg[a][:], u_ps[a], ALU.mult).then_inc(weighted, 1)
                    if j == 2 and not first:
                        add_y(n - 1, 1 - s)
                    stage(j)

            dve.sem_inc(weighted, 2)
            dve.sem_inc(y_ready, 2)
            dve.sem_inc(y_stored, 16)
            blocks(dve, prepare, expert_block)
            add_y(NBLK - 1, 1)


INPUTS = {
    "x": (B, SQ, D), "ctxT": (B, D, SK), "wqT": (D, D), "wkT": (D, D), "wvT": (D, D), "woT": (D, D),
    "bq": (D,), "bk": (D,), "bv": (D,), "bo": (D,), "gate_wT": (D, NE), "gate_bias": (NE,),
    "w_gateT": (D, NE * NI), "w_upT": (D, NE * NI), "w_downT": (P, UNITS * D),
    "sh_gateT": (D, P), "sh_upT": (D, P), "sh_downT": (P, D),
    "ident": (P, P), "pick": (P, 2, 4, VW), "spread": (3 * NE, UNITS, P),
}


def build(nc, io, out):
    ke = nc.dram_tensor("k_parts", (B, NH, PARTS, DH, SK), BF16).ap()
    qe = nc.dram_tensor("q_parts", (B, NH, NCOPY, DH, SQ), BF16).ap()
    ve = nc.dram_tensor("v_pairs", (B, PAIRS, P, NC * VC), F32).ap()
    with ExitStack() as ctx:
        sb = lambda name, shape, dt=F32: ctx.enter_context(nc.sbuf_tensor(name, shape, dt))
        att = sb("att", [P, B + 1, SQ])
        wh, wl = sb("wh", [P, PIECES * PIECE], F32R), sb("wl", [P, PIECES * PIECE], F32R)
        kept = Kept(sb)
        with ExitStack() as inner:
            operands = Operands(lambda name, shape, dt: inner.enter_context(nc.sbuf_tensor(name, shape, dt)),
                                lambda name: inner.enter_context(nc.semaphore(name)))
            project(nc, io, ke, qe, ve, kept, operands)
            attend(nc, io, ke, qe, ve, kept, operands, att, wh, wl)
        mix(nc, io, kept, att, wh, wl, out)


def constants():
    pick = np.zeros((P, 2, 4, VW), np.float32)
    for tile in range(CT):
        for half in range(2):
            for h in range(2):
                for d in range(DH):
                    pick[VW * tile + (DH + 1) * h + d, 0, 2 * half + h, 2 * DH * half + DH * h + d] = 1
                    pick[VW * tile + (DH + 1) * h + DH, 1, 2 * half + h, 2 * DH * half + DH * h + d] = 1
    spread = np.zeros((3 * NE, UNITS, P), np.float32)
    for r in range(3 * NE):
        for m in range(P):
            if (r % NE) % EPJ == m // NI:
                spread[r, (r % NE) // EPJ, m] = 1
    return {"ident": np.eye(P, dtype=np.float32), "pick": pick, "spread": spread}


def kernel(x, ctx_1024, L0_xattn_wq, L0_xattn_bq, L0_xattn_wk, L0_xattn_bk, L0_xattn_wv, L0_xattn_bv,
           L0_xattn_wo, L0_xattn_bo, L0_ffn_gate_w, L0_ffn_gate_bias, L0_ffn_w_gate, L0_ffn_w_up,
           L0_ffn_w_down, L0_ffn_sh_gate, L0_ffn_sh_up, L0_ffn_sh_down):
    import concourse.bacc as bacc
    from concourse.bass_utils import run_bass_kernel_spmd

    host = lambda a: np.asarray(a)
    given = {
        "x": host(x), "ctxT": host(ctx_1024).transpose(0, 2, 1),
        "wqT": host(L0_xattn_wq).T, "wkT": host(L0_xattn_wk).T, "wvT": host(L0_xattn_wv).T, "woT": host(L0_xattn_wo).T.reshape(2, CT, 2 * DH, D).transpose(1, 0, 2, 3).reshape(D, D),
        "bq": host(L0_xattn_bq), "bk": host(L0_xattn_bk), "bv": host(L0_xattn_bv), "bo": host(L0_xattn_bo),
        "gate_wT": host(L0_ffn_gate_w).T, "gate_bias": host(L0_ffn_gate_bias),
        "w_gateT": host(L0_ffn_w_gate).reshape(NE * NI, D).T, "w_upT": host(L0_ffn_w_up).reshape(NE * NI, D).T,
        "w_downT": host(L0_ffn_w_down).transpose(0, 2, 1).reshape(UNITS, P, D).transpose(1, 0, 2).reshape(P, UNITS * D),
        "sh_gateT": host(L0_ffn_sh_gate).T, "sh_upT": host(L0_ffn_sh_up).T, "sh_downT": host(L0_ffn_sh_down).T,
        **constants(),
    }
    nc = bacc.Bacc("TRN2", target_bir_lowering=False, num_devices=1)
    arrays, io = {}, {}
    for name, shape in INPUTS.items():
        a = np.ascontiguousarray(given[name])
        assert a.shape == shape, (name, a.shape)
        arrays[f"in_{name}"] = a
        io[name] = nc.dram_tensor(f"in_{name}", shape, mybir.dt.from_np(a.dtype), kind="ExternalInput").ap()
    out = nc.dram_tensor("out", (B, SQ, D), F32, kind="ExternalOutput").ap()
    build(nc, io, out)
    r = run_bass_kernel_spmd(nc, [arrays], core_ids=[0])
    return r.results[0]["out"]
```
